# Optimizing a Trainium2 kernel written in Bass

```python
import numpy as np
import jax
import jax.numpy as jnp

def _softmax(x, axis=-1):
    return jax.nn.softmax(x, axis=axis)

def _gelu(x):
    return jax.nn.gelu(x, approximate=True)

def _silu(x):
    return jax.nn.silu(x)

def _sigmoid(x):
    return jax.nn.sigmoid(x)

def _layernorm(x, axis=-1, eps=1e-05):
    m = jnp.mean(x, axis=axis, keepdims=True)
    v = jnp.var(x, axis=axis, keepdims=True)
    return (x - m) / jnp.sqrt(v + eps)

def _scatter_add(tgt, idx, src, axis=0):
    return tgt.at[idx].add(src)

def _segment_sum(src, seg, n):
    return jax.ops.segment_sum(src, seg, n)
kernel_name = 'mk_dlrm_tower_d1_rec_r8_927fab'

def setup_inputs(seed: int=0):
    np.random.seed(seed)
    _w = jnp.asarray

    def _rec_inputs():
        import jax
        import jax.numpy as jnp
        _tk = jax.random.key(seed)
        ids = jnp.stack([jax.random.randint(jax.random.fold_in(_tk, 200 + f), (2048,), 0, v, jnp.int32) for f, v in enumerate([1250, 125000, 1250, 1250, 1250, 1000, 1250, 1000, 12500, 1000, 1250, 1000, 1250, 1000, 1250, 12500, 12500, 12500, 12500, 12500, 1000, 1250, 12500, 1250, 1250, 1000])], axis=1)
        tbl_0 = 0.05 * jax.random.normal(jax.random.fold_in(_tk, 500 + 0), (1250, 128), jnp.float32)
        tbl_1 = 0.05 * jax.random.normal(jax.random.fold_in(_tk, 500 + 1), (125000, 128), jnp.float32)
        tbl_2 = 0.05 * jax.random.normal(jax.random.fold_in(_tk, 500 + 2), (1250, 128), jnp.float32)
        tbl_3 = 0.05 * jax.random.normal(jax.random.fold_in(_tk, 500 + 3), (1250, 128), jnp.float32)
        tbl_4 = 0.05 * jax.random.normal(jax.random.fold_in(_tk, 500 + 4), (1250, 128), jnp.float32)
        tbl_5 = 0.05 * jax.random.normal(jax.random.fold_in(_tk, 500 + 5), (1000, 128), jnp.float32)
        tbl_6 = 0.05 * jax.random.normal(jax.random.fold_in(_tk, 500 + 6), (1250, 128), jnp.float32)
        tbl_7 = 0.05 * jax.random.normal(jax.random.fold_in(_tk, 500 + 7), (1000, 128), jnp.float32)
        tbl_8 = 0.05 * jax.random.normal(jax.random.fold_in(_tk, 500 + 8), (12500, 128), jnp.float32)
        tbl_9 = 0.05 * jax.random.normal(jax.random.fold_in(_tk, 500 + 9), (1000, 128), jnp.float32)
        tbl_10 = 0.05 * jax.random.normal(jax.random.fold_in(_tk, 500 + 10), (1250, 128), jnp.float32)
        tbl_11 = 0.05 * jax.random.normal(jax.random.fold_in(_tk, 500 + 11), (1000, 128), jnp.float32)
        tbl_12 = 0.05 * jax.random.normal(jax.random.fold_in(_tk, 500 + 12), (1250, 128), jnp.float32)
        tbl_13 = 0.05 * jax.random.normal(jax.random.fold_in(_tk, 500 + 13), (1000, 128), jnp.float32)
        tbl_14 = 0.05 * jax.random.normal(jax.random.fold_in(_tk, 500 + 14), (1250, 128), jnp.float32)
        tbl_15 = 0.05 * jax.random.normal(jax.random.fold_in(_tk, 500 + 15), (12500, 128), jnp.float32)
        tbl_16 = 0.05 * jax.random.normal(jax.random.fold_in(_tk, 500 + 16), (12500, 128), jnp.float32)
        tbl_17 = 0.05 * jax.random.normal(jax.random.fold_in(_tk, 500 + 17), (12500, 128), jnp.float32)
        tbl_18 = 0.05 * jax.random.normal(jax.random.fold_in(_tk, 500 + 18), (12500, 128), jnp.float32)
        tbl_19 = 0.05 * jax.random.normal(jax.random.fold_in(_tk, 500 + 19), (12500, 128), jnp.float32)
        tbl_20 = 0.05 * jax.random.normal(jax.random.fold_in(_tk, 500 + 20), (1000, 128), jnp.float32)
        tbl_21 = 0.05 * jax.random.normal(jax.random.fold_in(_tk, 500 + 21), (1250, 128), jnp.float32)
        tbl_22 = 0.05 * jax.random.normal(jax.random.fold_in(_tk, 500 + 22), (12500, 128), jnp.float32)
        tbl_23 = 0.05 * jax.random.normal(jax.random.fold_in(_tk, 500 + 23), (1250, 128), jnp.float32)
        tbl_24 = 0.05 * jax.random.normal(jax.random.fold_in(_tk, 500 + 24), (1250, 128), jnp.float32)
        tbl_25 = 0.05 * jax.random.normal(jax.random.fold_in(_tk, 500 + 25), (1000, 128), jnp.float32)
        _rk = jax.random.fold_in(_tk, 7)
        r_dense_features = -0.000520686 + 1.00062 * jax.random.normal(jax.random.fold_in(_rk, 101), (2048, 128), jnp.float32)
        W_top1 = 0.0405887 * jax.random.normal(jax.random.fold_in(_tk, 801), (607, 512), jnp.float32)
        W_top2 = 0.0441942 * jax.random.normal(jax.random.fold_in(_tk, 802), (512, 256), jnp.float32)
        W_top3 = 0.0625 * jax.random.normal(jax.random.fold_in(_tk, 803), (256, 1), jnp.float32)
        b_top1 = jnp.zeros((512,), jnp.float32)
        b_top2 = jnp.zeros((256,), jnp.float32)
        return (r_dense_features, ids, tbl_0, tbl_1, tbl_2, tbl_3, tbl_4, tbl_5, tbl_6, tbl_7, tbl_8, tbl_9, tbl_10, tbl_11, tbl_12, tbl_13, tbl_14, tbl_15, tbl_16, tbl_17, tbl_18, tbl_19, tbl_20, tbl_21, tbl_22, tbl_23, tbl_24, tbl_25, W_top1, b_top1, W_top2, b_top2, W_top3)
    r_dense_features, ids, tbl_0, tbl_1, tbl_2, tbl_3, tbl_4, tbl_5, tbl_6, tbl_7, tbl_8, tbl_9, tbl_10, tbl_11, tbl_12, tbl_13, tbl_14, tbl_15, tbl_16, tbl_17, tbl_18, tbl_19, tbl_20, tbl_21, tbl_22, tbl_23, tbl_24, tbl_25, W_top1, b_top1, W_top2, b_top2, W_top3 = _rec_inputs()

    def _L0_rec_setup():
        import jax, jax.numpy as jnp
        import numpy as np
        F = 26
        N = F + 1
        _TRIU_I, _TRIU_J = np.triu_indices(N, k=1)
        key = jax.random.key(seed)
        k1, k2 = jax.random.split(key)
        B, D = (2048, 128)
        dense_features = jax.random.normal(k1, (B, D), dtype=jnp.float32)
        sparse_features = jax.random.normal(k2, (B, F, D), dtype=jnp.float32)
        return {'dense_features': dense_features, 'sparse_features': sparse_features}
    _L0_rec_all = _L0_rec_setup()
    _L0_rec_in = {k: v for k, v in _L0_rec_all.items() if k in ()}
    del _L0_rec_all
    return {'r_dense_features': r_dense_features, 'ids': ids, 'tbl_0': tbl_0, 'tbl_1': tbl_1, 'tbl_2': tbl_2, 'tbl_3': tbl_3, 'tbl_4': tbl_4, 'tbl_5': tbl_5, 'tbl_6': tbl_6, 'tbl_7': tbl_7, 'tbl_8': tbl_8, 'tbl_9': tbl_9, 'tbl_10': tbl_10, 'tbl_11': tbl_11, 'tbl_12': tbl_12, 'tbl_13': tbl_13, 'tbl_14': tbl_14, 'tbl_15': tbl_15, 'tbl_16': tbl_16, 'tbl_17': tbl_17, 'tbl_18': tbl_18, 'tbl_19': tbl_19, 'tbl_20': tbl_20, 'tbl_21': tbl_21, 'tbl_22': tbl_22, 'tbl_23': tbl_23, 'tbl_24': tbl_24, 'tbl_25': tbl_25, 'W_top1': W_top1, 'b_top1': b_top1, 'W_top2': W_top2, 'b_top2': b_top2, 'W_top3': W_top3}

def reference(r_dense_features, ids, tbl_0, tbl_1, tbl_2, tbl_3, tbl_4, tbl_5, tbl_6, tbl_7, tbl_8, tbl_9, tbl_10, tbl_11, tbl_12, tbl_13, tbl_14, tbl_15, tbl_16, tbl_17, tbl_18, tbl_19, tbl_20, tbl_21, tbl_22, tbl_23, tbl_24, tbl_25, W_top1, b_top1, W_top2, b_top2, W_top3):
    import jax
    import jax.numpy as jnp

    def _L0_rec_ref(dense_features, sparse_features):
        import jax, jax.numpy as jnp
        import numpy as np
        F = 26
        N = F + 1
        _TRIU_I, _TRIU_J = np.triu_indices(N, k=1)
        combined = jnp.concatenate([dense_features[:, None, :], sparse_features], axis=1)
        interactions = jnp.einsum('bnd,bmd->bnm', combined, combined)
        interactions_flat = interactions[:, _TRIU_I, _TRIU_J]
        return jnp.concatenate([dense_features, interactions_flat], axis=1)
    e = jnp.stack([tbl_0[ids[:, 0]], tbl_1[ids[:, 1]], tbl_2[ids[:, 2]], tbl_3[ids[:, 3]], tbl_4[ids[:, 4]], tbl_5[ids[:, 5]], tbl_6[ids[:, 6]], tbl_7[ids[:, 7]], tbl_8[ids[:, 8]], tbl_9[ids[:, 9]], tbl_10[ids[:, 10]], tbl_11[ids[:, 11]], tbl_12[ids[:, 12]], tbl_13[ids[:, 13]], tbl_14[ids[:, 14]], tbl_15[ids[:, 15]], tbl_16[ids[:, 16]], tbl_17[ids[:, 17]], tbl_18[ids[:, 18]], tbl_19[ids[:, 19]], tbl_20[ids[:, 20]], tbl_21[ids[:, 21]], tbl_22[ids[:, 22]], tbl_23[ids[:, 23]], tbl_24[ids[:, 24]], tbl_25[ids[:, 25]]], axis=1)
    z = _L0_rec_ref(r_dense_features, e)
    z = z.reshape(z.shape[0], -1)
    h = jnp.concatenate([z, r_dense_features], axis=1)
    h = jnp.maximum(h @ W_top1 + b_top1, 0.0)
    h = jnp.maximum(h @ W_top2 + b_top2, 0.0)
    y = h @ W_top3
    return y

_drawn_inputs = setup_inputs


def setup_inputs(seed=0):
    import zlib

    import numpy as np

    out = dict(_drawn_inputs(seed))
    spreads = {'b_top1': (0.0, 0.1), 'b_top2': (0.0, 0.1)}
    factors = {}
    for name, (base, spread) in spreads.items():
        noise = np.random.default_rng([zlib.crc32(name.encode()), seed]).standard_normal(out[name].shape)
        drawn = base * np.exp(spread * noise) if base else spread * noise
        out[name] = jnp.asarray(drawn.astype(out[name].dtype))
    for name, factor in factors.items():
        out[name] = (out[name] * factor).astype(out[name].dtype)
    return out
```

```python
from contextlib import ExitStack

import numpy as np

import concourse.bass as bass
from concourse import mybir

ALU = mybir.AluOpType
ACT = mybir.ActivationFunctionType
F32 = mybir.dt.float32
F32R = mybir.dt.float32r
I32 = mybir.dt.int32

B, D, TABLES = 2048, 128, 26
NODES = TABLES + 1
P = 128
TILE = 128
HALF = 2 * TILE
PAIR = 2 * HALF
TILES, HALVES, PAIRS = B // TILE, B // HALF, B // PAIR
QUAD = 4
SLOT = P // QUAD
GROUPS = PAIR // QUAD
NPAIRS = NODES * (NODES - 1) // 2
ZROWS = 117
ZSLICES = NPAIRS // ZROWS
H1, H2 = 512, 256
ROWS = 125

ONE_HOT = [5, 7, 9, 11, 13, 20, 25, 0]
GATHERED = [f for f in range(TABLES) if f not in ONE_HOT]
NG, NO = len(GATHERED), len(ONE_HOT)
ORDER = [0] + [1 + f for f in GATHERED] + [1 + f for f in ONE_HOT]
NROWS = 1 + NG
TGROUPS = -(-NROWS // 4)
QBANKS = TILE // QUAD // 4
GTBANKS = -(-(NODES - 1) // 4)
MAXSLICE = 5
ONE_HOT_SLOTS = 4


def pair_start(n):
    return n * (2 * NODES - n - 1) // 2


STEPS = ([("turn", q) for q in range(GTBANKS)] + [("pairs", c) for c in range(ZSLICES)]
         + [("layer1", m) for m in range(H1 // P)] + [("layer2", m) for m in range(H2 // P)] + [("layer3", 0)])
STEP_AT = {step: i for i, step in enumerate(STEPS)}
AFTER_UNIT = {0: STEPS[0:2], 1: STEPS[2:4], 2: STEPS[4:6], 3: STEPS[6:7], 4: STEPS[7:10], 5: STEPS[10:14],
              6: STEPS[14:16], 7: STEPS[16:17]}


def build(nc, dense, ids_rows, ids_cols, tables, w1, w2, vectors, y):
    slices = [tables[f].shape[0] // ROWS for f in ONE_HOT]
    assert all(tables[f].shape[0] == ROWS * n for f, n in zip(ONE_HOT, slices)) and NO % 2 == 0
    assert ZROWS * ZSLICES == NPAIRS and TGROUPS % 2 == 1 and len(STEPS) % 2 == 1

    with ExitStack() as ctx:
        def sb(name, shape, dt=F32):
            return ctx.enter_context(nc.sbuf_tensor(name, shape, dt))

        def bank(name):
            return ctx.enter_context(nc.psum_tensor(name, [P, 512], F32))

        def sem(name):
            return ctx.enter_context(nc.semaphore(name))

        ident = sb("ident", [P, P])
        row_number_i = sb("row_number_i", [P, 2, max(slices)], I32)
        row_number = sb("row_number", [P, 2, max(slices)])
        index = sb("index", [P, TILES * NG], I32)
        index_now = sb("index_now", [P, 4, NG], I32)
        w1d = sb("w1d", [P, H1])
        w1z = sb("w1z", [ZROWS, ZSLICES, H1])
        w2s = sb("w2s", [P, H1 // P, H2])
        columns = sb("columns", [P, (H1 + 2 * H2) // P])
        b1s, b2s, w3s = (columns[:, a // P:b // P] for a, b in ((0, H1), (H1, H1 + H2), (H1 + H2, H1 + 2 * H2)))
        part_hi = [sb(f"part_hi{u}", [ROWS, n, D], F32R) for u, n in enumerate(slices)]
        part_lo = [sb(f"part_lo{u}", [ROWS, n, D], F32R) for u, n in enumerate(slices)]
        carrier = sb("carrier", [P, 1], I32)
        rows = sb("rows", [P, 4, NROWS, D])
        ids_all = sb("ids_all", [P, NO, HALF], I32)
        one_hot = sb("one_hot", [ROWS, ONE_HOT_SLOTS, MAXSLICE, HALF], F32R)
        features = sb("features", [P, HALF, SLOT])
        dense_t = sb("dense_t", [P, QUAD, GROUPS])
        products = sb("products", [P, NODES, GROUPS])
        by_sample = sb("by_sample", [P, QUAD, NPAIRS])
        by_pair = sb("by_pair", [P, ZSLICES, PAIR])
        ys = sb("ys", [P, PAIRS * QUAD])
        flat = products[:].rearrange("p n g -> p (n g)")
        h1 = flat[:, 0:H1 // P * PAIR].rearrange("p (m s) -> p m s", s=PAIR)
        h2 = flat[:, H1 // P * PAIR:(H1 + H2) // P * PAIR].rearrange("p (m s) -> p m s", s=PAIR)
        stage = ([flat[0:ROWS, i * 1024:(i + 1) * 1024] for i in range(3)]
                 + [by_pair[:].rearrange("p c s -> p (c s)")[0:ROWS, 0:1024],
                    by_sample[:].rearrange("p j n -> p (j n)")[0:ROWS, 0:1280]])
        spots = [0, 1, 2, 3, 0, 1, 2, 4]
        b_rows_stage = dense_t[:].rearrange("p j g -> p (j g)")

        rows_ps = [bank(f"rows_ps{i}") for i in range(2)]
        lookup_ps = [bank(f"lookup_ps{i}") for i in range(2)]
        gram_ps = [bank(f"gram_ps{i}") for i in range(2)]
        mlp_ps = [bank(f"mlp_ps{i}") for i in range(2)]

        index_landed = sem("index_landed")
        raw_landed = [sem(f"raw_landed{u}") for u in range(NO)]
        ids_landed = [sem(f"ids_landed{u}") for u in range(NO)]
        dense_landed = [sem(f"dense_landed{i}") for i in range(4)]
        rows_landed = [sem(f"rows_landed{i}") for i in range(4)]
        w1d_landed = sem("w1d_landed")
        weights_landed = sem("weights_landed")
        y_stored = sem("y_stored")
        cleared = sem("cleared")
        ident_ready = sem("ident_ready")
        iota_ready = sem("iota_ready")
        index_ready = sem("index_ready")
        row_number_ready = sem("row_number_ready")
        padding_ready = sem("padding_ready")
        lo_ready = sem("lo_ready")
        w1d_ready = sem("w1d_ready")
        one_hot_ready = sem("one_hot_ready")
        turn_copied = sem("turn_copied")
        y_copied = sem("y_copied")
        hi_ready = sem("hi_ready")
        lookup_copied = sem("lookup_copied")
        gram_copied = sem("gram_copied")
        pairs_copied = sem("pairs_copied")
        h1_ready = sem("h1_ready")
        h2_ready = sem("h2_ready")
        rows_copied = [sem("rows_copied_act"), sem("rows_copied_dve")]
        one_hot_used = sem("one_hot_used")
        rows_turned = sem("rows_turned")
        gram_done = sem("gram_done")
        step_done = {kind: sem(f"{kind}_done") for kind in ("turn", "pairs", "layer1", "layer2", "layer3")}
        per_pair = {"turn": GTBANKS, "pairs": ZSLICES, "layer1": H1 // P, "layer2": H2 // P, "layer3": 1}
        step_copied = {"turn": turn_copied, "pairs": pairs_copied, "layer1": h1_ready, "layer2": h2_ready,
                       "layer3": y_copied}

        def granule(u, part):
            n = slices[u] // 2
            return range(part * n, (part + 1) * n)

        def copy_rows(engine, copy, side, pair, slot, first):
            s = slot % 2
            for q in range(TGROUPS):
                i = slot * TGROUPS + q
                if i % 2 != side:
                    continue
                engine.wait_ge(rows_turned, (pair * 4 + slot) * TGROUPS + (q + 1))
                n0, n1 = 4 * q, min(4 * q + 4, NROWS)
                src = rows_ps[side][:, 0:(n1 - n0) * P]
                if q == 0:
                    if first:
                        engine.wait_ge(w1d_ready, 1)
                    g = slot * (TILE // QUAD)
                    copy(dense_t[:, :, g:g + TILE // QUAD], src[:, 0:P].rearrange("p (g j) -> p j g", j=QUAD))
                copy(features[:, s * TILE:(s + 1) * TILE, n0:n1],
                     src.rearrange("p (n b) -> p b n", b=P)).then_inc(rows_copied[side], 1)

        block = ctx.enter_context(nc.Block())

        def over_pairs(engine, body):
            body(0, True, False)
            with engine.Fori(1, PAIRS - 1) as pair:
                body(pair, False, False)
            body(PAIRS - 1, False, True)

        @block.sync
        def _(sp):
            def load_table(u):
                raw = tables[ONE_HOT[u]].rearrange("(p c) d -> p (c d)", p=ROWS)
                dst = stage[spots[u]][:, 0:slices[u] * D]
                sp.dma_start(dst[0:112, :], raw[0:112, :]).then_inc(raw_landed[u], 16)
                sp.dma_start(dst[112:ROWS, :], raw[112:ROWS, :]).then_inc(raw_landed[u], 16)

            def load_ids(half, u):
                sp.dma_start(ids_all[:, u, :], ids_rows[half, u, :].partition_broadcast(P)).then_inc(ids_landed[u], 16)

            def load_dense(tile, slot):
                sp.dma_start(rows[:, slot, 0, :], dense[tile, :, :]).then_inc(dense_landed[slot], 16)

            sp.dma_start(index[:], ids_cols).then_inc(index_landed, 16)
            order = sorted(range(NO), key=lambda u: spots[:u].count(spots[u]))
            for u in order:
                if spots[u] in spots[:u]:
                    sp.wait_ge(lo_ready, spots.index(spots[u]) + 1)
                load_table(u)
                load_ids(0, u)
            sp.dma_start(w1d[:], w1[0:D, :]).then_inc(w1d_landed, 16)
            sp.dma_start(b_rows_stage, w1[D + NPAIRS:, :]).then_inc(w1d_landed, 16)
            for slot in range(4):
                load_dense(slot, slot)
            sp.dma_start(w1z[:], w1[D:D + NPAIRS, :].rearrange("(c p) n -> p c n", p=ZROWS)).then_inc(weights_landed, 16)
            sp.dma_start(w2s[:], w2.rearrange("(c p) n -> p c n", p=P)).then_inc(weights_landed, 16)
            sp.dma_start(columns[:], vectors).then_inc(weights_landed, 16)

            def body(pair, first, last):
                for hh in range(2):
                    half = pair * 2 + hh
                    if not (last and hh == 1):
                        for u in range(NO):
                            sp.wait_ge(one_hot_ready, half * (2 * NO) + 2 * u + 2)
                            load_ids(half + 1, u)
                    if not last:
                        for s in range(2):
                            tile = pair * 4 + (2 * hh + s)
                            sp.wait_ge(rows_turned, tile * TGROUPS + TGROUPS)
                            load_dense(tile + 4, 2 * hh + s)

            over_pairs(sp, body)
            sp.wait_ge(y_copied, PAIRS)
            sp.dma_start(y.rearrange("(q g j) o -> g q (j o)", q=PAIRS, j=QUAD),
                         ys[:].rearrange("g (q j) -> g q j", j=QUAD)).then_inc(y_stored, 16)
            sp.wait_ge(y_stored, 16)

        @block.gpsimd
        def _(pool):
            for kind, n in enumerate((min(slices), max(slices))):
                nc.gpsimd.iota(row_number_i[:, kind, 0:n], [[1, n]], base=0, channel_multiplier=n).then_inc(iota_ready, 1)
            nc.gpsimd.memset(ident[:], 0.0).then_inc(cleared, 1)
            pool.wait_ge(cleared, 1)
            nc.gpsimd.affine_select(out=ident[:], in_=ident[:], compare_op=ALU.not_equal, fill=1.0, base=0,
                                    pattern=[[-1, P]], channel_multiplier=1).then_inc(ident_ready, 1)
            pool.wait_ge(index_landed, 16)

            def body(pair, first, last):
                for slot in range(4):
                    tile = pair * 4 + slot
                    if not first:
                        pool.wait_ge(rows_turned, (tile - 4) * TGROUPS + TGROUPS)
                    nc.gpsimd.tensor_copy(index_now[:, slot, :], index[:, bass.ds(tile * NG, NG)]).then_inc(index_ready, 1)
                    pool.wait_ge(index_ready, tile + 1)
                    nc.gpsimd.tensor_tensor(carrier[:], index_now[:, slot, 0:1], index_now[:, slot, 0:1], ALU.add)
                    for i, f in enumerate(GATHERED):
                        nc.gpsimd.indirect_dma_start(
                            rows[:, slot, 1 + i, :], None, tables[f],
                            bass.IndirectOffsetOnAxis(ap=index_now[:, slot, i:i + 1], axis=0),
                        ).then_inc(rows_landed[slot], 16)

            over_pairs(nc.gpsimd, body)

        @block.tensor
        def _(pe):
            def lookup(pair, hh, u, first):
                half = pair * 2 + hh
                b = (hh * NO + u) % 2
                out = lookup_ps[b][:, 0:HALF]
                if first and hh == 0:
                    pe.wait_ge(hi_ready, u + 1)
                    pe.wait_ge(lo_ready, u + 1)
                if not (first and hh == 0 and u < 2):
                    pe.wait_ge(lookup_copied, half * NO + (u - 1))
                for part in range(2):
                    pe.wait_ge(one_hot_ready, half * (2 * NO) + (2 * u + part + 1))
                    for c in granule(u, part):
                        for table in (part_hi[u], part_lo[u]):
                            mm = nc.tensor.matmul(out, table[:, c, :],
                                                  one_hot[:, (2 * u + part) % ONE_HOT_SLOTS, c - granule(u, part)[0], :],
                                                  start=(c == 0 and table is part_hi[u]),
                                                  stop=(c == slices[u] - 1 and table is part_lo[u]))
                    mm.then_inc(one_hot_used, 1)

            def turn_rows(pair, slot, first):
                pe.wait_ge(rows_landed[slot], pair * (16 * NG) + 16 * NG)
                pe.wait_ge(dense_landed[slot], pair * 16 + 16)
                for q in range(TGROUPS):
                    i = slot * TGROUPS + q
                    if not (first and i < 2):
                        pe.wait_ge(rows_copied[i % 2], pair * (2 * TGROUPS) + i // 2)
                    for n in range(4 * q, min(4 * q + 4, NROWS)):
                        mm = nc.tensor.transpose(rows_ps[i % 2][:, (n % 4) * P:(n % 4 + 1) * P],
                                                 rows[:, slot, n, :], ident[:])
                    mm.then_inc(rows_turned, 1)

            def products_of(pair, slot, first):
                hh, s = divmod(slot, 2)
                pe.wait_ge(rows_copied[0], pair * (2 * TGROUPS) + ((slot + 1) * TGROUPS + 1) // 2)
                pe.wait_ge(rows_copied[1], pair * (2 * TGROUPS) + (slot + 1) * TGROUPS // 2)
                if s == 0:
                    pe.wait_ge(lookup_copied, (pair * 2 + hh) * NO + NO)
                for r in range(QBANKS):
                    if not (first and slot == 0 and r < 2):
                        pe.wait_ge(gram_copied, (pair * 4 + slot) * QBANKS + (r - 1))
                    for w in range(4):
                        c = s * TILE + (4 * r + w) * QUAD
                        mm = nc.tensor.matmul(gram_ps[r % 2][:, w * QUAD * NODES:(w + 1) * QUAD * NODES],
                                              features[:, c:c + QUAD, :], features[:, c:c + QUAD, 0:NODES],
                                              start=True, stop=True)
                    mm.then_inc(gram_done, 1)

            def step(pair, kind, n, first):
                i = STEP_AT[kind, n]
                out = mlp_ps[i % 2]
                before = i - 2 if i >= 2 else (len(STEPS) - 1 if i == 0 else len(STEPS) - 2)
                if i >= 2:
                    bk, bn = STEPS[before]
                    pe.wait_ge(step_copied[bk], pair * per_pair[bk] + (bn + 1))
                elif not first:
                    bk, bn = STEPS[before]
                    pe.wait_ge(step_copied[bk], (pair - 1) * per_pair[bk] + (bn + 1))
                if kind == "turn":
                    if n == 0:
                        pe.wait_ge(gram_copied, pair * (4 * QBANKS) + 4 * QBANKS)
                    for m in range(4 * n, min(4 * n + 4, NODES - 1)):
                        mm = nc.tensor.transpose(out[:, (m % 4) * P:(m % 4 + 1) * P], products[:, m, :], ident[:])
                elif kind == "pairs":
                    if n == 0:
                        pe.wait_ge(turn_copied, pair * GTBANKS + GTBANKS)
                    for j in range(QUAD):
                        mm = nc.tensor.transpose(out[0:ZROWS, j * P:(j + 1) * P],
                                                 by_sample[:, j, n * ZROWS:(n + 1) * ZROWS], ident[:])
                elif kind == "layer1":
                    if n == 0:
                        pe.wait_ge(pairs_copied, pair * ZSLICES + ZSLICES)
                        if first:
                            pe.wait_ge(w1d_ready, 1)
                            pe.wait_ge(weights_landed, 48)
                    mm = nc.tensor.matmul(out[:], w1d[:, n * P:(n + 1) * P],
                                          dense_t[:].rearrange("p j g -> p (j g)"), start=True, stop=False)
                    for c in range(ZSLICES):
                        mm = nc.tensor.matmul(out[:], w1z[:, c, n * P:(n + 1) * P], by_pair[0:ZROWS, c, :],
                                              start=False, stop=(c == ZSLICES - 1))
                elif kind == "layer2":
                    if n == 0:
                        pe.wait_ge(h1_ready, pair * (H1 // P) + H1 // P)
                    for c in range(H1 // P):
                        mm = nc.tensor.matmul(out[:], w2s[:, c, n * P:(n + 1) * P], h1[:, c, :],
                                              start=(c == 0), stop=(c == H1 // P - 1))
                else:
                    pe.wait_ge(h2_ready, pair * (H2 // P) + H2 // P)
                    for j in range(QUAD):
                        for c in range(H2 // P):
                            mm = nc.tensor.matmul(out[:, j:j + 1], h2[:, c, j * GROUPS:(j + 1) * GROUPS],
                                                  w3s[:, c:c + 1], start=(c == 0), stop=(c == H2 // P - 1))
                mm.then_inc(step_done[kind], 1)

            pe.wait_ge(ident_ready, 1)
            pe.wait_ge(padding_ready, 1)

            def body(pair, first, second):
                for hh in range(2):
                    for u in range(NO):
                        lookup(pair, hh, u, first)
                        if hh == 0 and not first:
                            for kind, n in AFTER_UNIT[u]:
                                step(pair - 1, kind, n, second)
                    for s in range(2):
                        turn_rows(pair, 2 * hh + s, first)
                        products_of(pair, 2 * hh + s, first)

            body(0, True, False)
            body(1, False, True)
            with nc.tensor.Fori(2, PAIRS) as pair:
                body(pair, False, False)
            for kind, n in STEPS:
                step(PAIRS - 1, kind, n, False)

        @block.scalar
        def _(act):
            for u in range(NO):
                act.wait_ge(raw_landed[u], 32)
                nc.scalar.copy(part_hi[u][:].rearrange("p c d -> p (c d)"),
                               stage[spots[u]][:, 0:slices[u] * D]).then_inc(hi_ready, 1)

            def step(pair, kind, n, first):
                if kind not in ("pairs", "layer1", "layer2"):
                    return
                src = mlp_ps[STEP_AT[kind, n] % 2]
                act.wait_ge(step_done[kind], pair * per_pair[kind] + (n + 1))
                if kind == "pairs":
                    nc.scalar.copy(by_pair[0:ZROWS, n, :], src[0:ZROWS, :]).then_inc(pairs_copied, 1)
                elif kind == "layer1":
                    if n == 0 and first:
                        act.wait_ge(weights_landed, 48)
                    nc.scalar.activation(h1[:, n, :], src[:], ACT.Relu, bias=b1s[:, n:n + 1]).then_inc(h1_ready, 1)
                else:
                    nc.scalar.activation(h2[:, n, :], src[:], ACT.Relu, bias=b2s[:, n:n + 1]).then_inc(h2_ready, 1)

            def body(pair, first, second):
                for hh in range(2):
                    half = pair * 2 + hh
                    for u in range(NO):
                        act.wait_ge(one_hot_used, half * (2 * NO) + 2 * u + 2)
                        if first and hh == 0 and u == 0:
                            act.wait_ge(padding_ready, 1)
                        nc.scalar.copy(features[:, :, NROWS + u], lookup_ps[(hh * NO + u) % 2][:, 0:HALF])\
                          .then_inc(lookup_copied, 1)
                        if hh == 0 and not first:
                            for kind, n in AFTER_UNIT[u]:
                                step(pair - 1, kind, n, second)
                    for s in range(2):
                        slot = 2 * hh + s
                        copy_rows(act, nc.scalar.copy, 0, pair, slot, first)
                        for r in range(QBANKS):
                            act.wait_ge(gram_done, (pair * 4 + slot) * QBANKS + (r + 1))
                            if first and slot == 0 and r == 0:
                                act.wait_ge(lo_ready, NO)
                            g = slot * (TILE // QUAD) + 4 * r
                            for j in range(QUAD):
                                part = slice(j * SLOT, j * SLOT + NODES)
                                src = gram_ps[r % 2][part, 0:4 * QUAD * NODES].rearrange(
                                    "p (w i m) -> p i m w", w=4, i=QUAD)[:, j, :, :]
                                ev = nc.scalar.copy(products[part, :, g:g + 4], src)
                            ev.then_inc(gram_copied, 1)

            body(0, True, False)
            body(1, False, True)
            with nc.scalar.Fori(2, PAIRS) as pair:
                body(pair, False, False)
            for kind, n in STEPS:
                step(PAIRS - 1, kind, n, False)

        @block.vector
        def _(dve):
            nc.vector.memset(features[:, :, NODES:SLOT], 0.0).then_inc(padding_ready, 1)
            dve.wait_ge(iota_ready, 2)
            for kind, n in enumerate((min(slices), max(slices))):
                nc.vector.tensor_copy(row_number[:, kind, 0:n], row_number_i[:, kind, 0:n])\
                  .then_inc(row_number_ready, 1)

            def split(u):
                dve.wait_ge(raw_landed[u], 32)
                dve.wait_ge(hi_ready, u + 1)
                nc.vector.tensor_tensor(part_lo[u][:].rearrange("p c d -> p (c d)"), stage[spots[u]][:, 0:slices[u] * D],
                                        part_hi[u][:].rearrange("p c d -> p (c d)").bitcast(F32),
                                        ALU.subtract).then_inc(lo_ready, 1)

            def make_one_hot(half, u, wait_used):
                kind = int(slices[u] != min(slices))
                dve.wait_ge(ids_landed[u], half * 16 + 16)
                for part in range(2):
                    if wait_used:
                        dve.wait_ge(one_hot_used, half * (2 * NO) + (2 * u + part + 1 - ONE_HOT_SLOTS))
                    for c in granule(u, part):
                        ins = nc.vector.tensor_scalar(
                            one_hot[:, (2 * u + part) % ONE_HOT_SLOTS, c - granule(u, part)[0], :],
                            ids_all[0:ROWS, u, :], row_number[0:ROWS, kind, c:c + 1], None, ALU.is_equal)
                    ins.then_inc(one_hot_ready, 1)

            dve.wait_ge(row_number_ready, 2)
            for u in range(2):
                split(u)
                make_one_hot(0, u, False)

            def step(pair, kind, n):
                src = mlp_ps[STEP_AT[kind, n] % 2]
                if kind == "turn":
                    dve.wait_ge(step_done[kind], pair * GTBANKS + (n + 1))
                    for m in range(4 * n, min(4 * n + 4, NODES - 1)):
                        ins = nc.vector.tensor_copy(
                            by_sample[:, :, pair_start(m):pair_start(m + 1)],
                            src[:, (m % 4) * P:(m % 4 + 1) * P].rearrange("p (j n) -> p j n", n=SLOT)[:, :, m + 1:NODES])
                    ins.then_inc(turn_copied, 1)
                elif kind == "layer3":
                    dve.wait_ge(step_done[kind], pair + 1)
                    nc.vector.tensor_copy(ys[:, bass.ds(pair * QUAD, QUAD)], src[:, 0:QUAD]).then_inc(y_copied, 1)

            def body(pair, first, last):
                for hh in range(2):
                    half = pair * 2 + hh
                    for u in range(NO):
                        if hh == 0 and not first:
                            for kind, n in AFTER_UNIT[u]:
                                step(pair - 1, kind, n)
                        if u + 2 < NO:
                            if first and hh == 0:
                                split(u + 2)
                            make_one_hot(half, u + 2, True)
                    if first and hh == 0:
                        dve.wait_ge(w1d_landed, 32)
                        nc.vector.tensor_tensor(w1d[:], w1d[:], b_rows_stage, ALU.add).then_inc(w1d_ready, 1)
                    for s in range(2):
                        copy_rows(dve, nc.vector.tensor_copy, 1, pair, 2 * hh + s, first)
                    if not (last and hh == 1):
                        for u in range(2):
                            make_one_hot(half + 1, u, True)

            over_pairs(nc.vector, body)
            for kind, n in STEPS:
                step(PAIRS - 1, kind, n)


def kernel(**inputs):
    import concourse.bacc as bacc
    from concourse.bass_utils import run_bass_kernel_spmd

    nc = bacc.Bacc("TRN2", target_bir_lowering=False, num_devices=1)
    arrays = {}

    def given(name, a):
        a = np.ascontiguousarray(a)
        arrays[f"in_{name}"] = a
        return nc.dram_tensor(f"in_{name}", a.shape, mybir.dt.from_np(a.dtype), kind="ExternalInput").ap()

    ids = np.asarray(inputs["ids"])
    w1 = np.asarray(inputs["W_top1"])
    place = {}
    for a in range(NODES):
        for b in range(a + 1, NODES):
            place[a, b] = D + pair_start(a) + b - a - 1
    pair_rows = [place[min(ORDER[a], ORDER[b]), max(ORDER[a], ORDER[b])]
                 for a in range(NODES) for b in range(a + 1, NODES)]
    w1_order = list(range(D)) + pair_rows + list(range(D + NPAIRS, 2 * D + NPAIRS))
    build(
        nc,
        given("dense", np.asarray(inputs["r_dense_features"]).reshape(TILES, TILE, D)),
        given("ids_rows", ids[:, ONE_HOT].reshape(HALVES, HALF, NO).transpose(0, 2, 1)),
        given("ids_cols", ids[:, GATHERED].reshape(TILES, TILE, NG).transpose(1, 0, 2).reshape(TILE, TILES * NG)),
        [given(f"tbl_{f}", inputs[f"tbl_{f}"]) for f in range(TABLES)],
        given("w1", w1[w1_order]),
        given("w2", inputs["W_top2"]),
        given("vectors", np.concatenate([np.asarray(inputs[n]).reshape(-1, P).T
                                         for n in ("b_top1", "b_top2", "W_top3")], axis=1)),
        nc.dram_tensor("out_y", (B, 1), F32, kind="ExternalOutput").ap(),
    )
    return run_bass_kernel_spmd(nc, [arrays], core_ids=[0]).results[0]["out_y"]
```

```python
from contextlib import ExitStack

import numpy as np

import concourse.bass as bass
from concourse import mybir

ALU = mybir.AluOpType
ACT = mybir.ActivationFunctionType
F32 = mybir.dt.float32
F32R = mybir.dt.float32r
I32 = mybir.dt.int32

B, D, TABLES = 2048, 128, 26
NODES = TABLES + 1
P = 128
TILE = 128
HALF = 2 * TILE
PAIR = 2 * HALF
TILES, HALVES, PAIRS = B // TILE, B // HALF, B // PAIR
QUAD = 4
SLOT = P // QUAD
GROUPS = PAIR // QUAD
NPAIRS = NODES * (NODES - 1) // 2
ZROWS = 117
ZSLICES = NPAIRS // ZROWS
H1, H2 = 512, 256
ROWS = 125
SPRAY = 112

ONE_HOT = [5, 7, 9, 11, 13, 20, 25, 0]
GATHERED = [f for f in range(TABLES) if f not in ONE_HOT]
NG, NO = len(GATHERED), len(ONE_HOT)
ORDER = [0] + [1 + f for f in GATHERED] + [1 + f for f in ONE_HOT]
NROWS = 1 + NG
TGROUPS = -(-NROWS // 4)
QBANKS = TILE // QUAD // 4
GRAM_SIDE = [0, 1, 0, 0]
GTBANKS = -(-(NODES - 1) // 4)
MAXSLICE = 5
ONE_HOT_SLOTS = 4


def pair_start(n):
    return n * (2 * NODES - n - 1) // 2


STEPS = ([("turn", q) for q in range(GTBANKS)] + [("pairs", c) for c in range(ZSLICES)]
         + [("layer1", m) for m in range(H1 // P)] + [("layer2", m) for m in range(H2 // P)] + [("layer3", 0)])
STEP_AT = {step: i for i, step in enumerate(STEPS)}
AFTER_UNIT = {0: STEPS[0:2], 1: STEPS[2:4], 2: STEPS[4:6], 3: STEPS[6:7], 4: STEPS[7:10], 5: STEPS[10:14],
              6: STEPS[14:16], 7: STEPS[16:17]}


def build(nc, dense, dense_cols, ids_rows, ids_cols, tables, w1, w2, vectors, y):
    slices = [tables[f].shape[0] // ROWS for f in ONE_HOT]
    assert all(tables[f].shape[0] == ROWS * n for f, n in zip(ONE_HOT, slices)) and NO % 2 == 0
    assert ZROWS * ZSLICES == NPAIRS and TGROUPS % 2 == 1 and len(STEPS) % 2 == 1

    with ExitStack() as ctx:
        def sb(name, shape, dt=F32):
            return ctx.enter_context(nc.sbuf_tensor(name, shape, dt))

        def bank(name):
            return ctx.enter_context(nc.psum_tensor(name, [P, 512], F32))

        def sem(name):
            return ctx.enter_context(nc.semaphore(name))

        ident = sb("ident", [P, P])
        row_number_i = sb("row_number_i", [P, 2, max(slices)], I32)
        row_number = sb("row_number", [P, 2, max(slices)])
        index = sb("index", [P, TILES * NG], I32)
        index_now = sb("index_now", [P, 4, NG], I32)
        w1d = sb("w1d", [P, H1])
        w1z = sb("w1z", [ZROWS, ZSLICES, H1])
        w2s = sb("w2s", [P, H1 // P, H2])
        columns = sb("columns", [P, (H1 + 2 * H2) // P])
        b1s, b2s, w3s = (columns[:, a // P:b // P] for a, b in ((0, H1), (H1, H1 + H2), (H1 + H2, H1 + 2 * H2)))
        part_hi = [sb(f"part_hi{u}", [ROWS, n, D], F32R) for u, n in enumerate(slices)]
        part_lo = [sb(f"part_lo{u}", [ROWS, n, D], F32R) for u, n in enumerate(slices)]
        carrier = sb("carrier", [P, 1], I32)
        rows = sb("rows", [P, 4, NROWS, D])
        ids_all = sb("ids_all", [P, NO, HALF], I32)
        one_hot = sb("one_hot", [ROWS, ONE_HOT_SLOTS, MAXSLICE, HALF], F32R)
        features = sb("features", [P, HALF, SLOT])
        dense_t = sb("dense_t", [P, PAIR])
        products = sb("products", [P, NODES, GROUPS])
        by_sample = sb("by_sample", [P, QUAD, NPAIRS])
        by_pair = sb("by_pair", [P, ZSLICES, PAIR])
        ys = sb("ys", [P, PAIRS * QUAD])
        flat = products[:].rearrange("p n g -> p (n g)")
        h1 = flat[:, 0:H1 // P * PAIR].rearrange("p (m s) -> p m s", s=PAIR)
        h2 = flat[:, H1 // P * PAIR:(H1 + H2) // P * PAIR].rearrange("p (m s) -> p m s", s=PAIR)
        late_rows = [rows[:, slot, :, :].rearrange("p n d -> p (n d)") for slot in (2, 3)]
        stage = [area[0:ROWS, at:at + n * D] for n, (area, at) in zip(slices, (
            (flat, 0), (flat, 1024), (flat, 2048), (by_pair[:].rearrange("p c s -> p (c s)"), 0),
            (late_rows[0], 0), (late_rows[1], 0), (late_rows[1], 1024),
            (by_sample[:].rearrange("p j n -> p (j n)"), 0)))]

        rows_ps = [bank(f"rows_ps{i}") for i in range(2)]
        lookup_ps = [bank(f"lookup_ps{i}") for i in range(2)]
        gram_ps = [bank(f"gram_ps{i}") for i in range(2)]
        mlp_ps = [bank(f"mlp_ps{i}") for i in range(2)]
        gram_ring = gram_ps + mlp_ps

        index_landed = sem("index_landed")
        raw_landed = [sem(f"raw_landed{u}") for u in range(NO)]
        ids_landed = [sem(f"ids_landed{u}") for u in range(NO)]
        dense_landed = [sem(f"dense_landed{i}") for i in range(4)]
        rows_landed = [sem(f"rows_landed{i}") for i in range(4)]
        w1d_landed = sem("w1d_landed")
        dense_t_landed = sem("dense_t_landed")
        weights_landed = sem("weights_landed")
        y_stored = sem("y_stored")
        cleared = sem("cleared")
        ident_ready = sem("ident_ready")
        iota_ready = sem("iota_ready")
        index_ready = sem("index_ready")
        row_number_ready = sem("row_number_ready")
        padding_ready = sem("padding_ready")
        lo_ready = sem("lo_ready")
        w1d_ready = sem("w1d_ready")
        one_hot_ready = sem("one_hot_ready")
        turn_copied = sem("turn_copied")
        y_copied = sem("y_copied")
        hi_ready = sem("hi_ready")
        lookup_copied = sem("lookup_copied")
        pairs_copied = sem("pairs_copied")
        h1_ready = sem("h1_ready")
        h2_ready = sem("h2_ready")
        rows_copied = sem("rows_copied")
        gram_copied = [sem("gram_copied_act"), sem("gram_copied_dve")]
        one_hot_used = sem("one_hot_used")
        rows_turned = sem("rows_turned")
        gram_done = sem("gram_done")
        step_done = {kind: sem(f"{kind}_done") for kind in ("turn", "pairs", "layer1", "layer2", "layer3")}
        per_pair = {"turn": GTBANKS, "pairs": ZSLICES, "layer1": H1 // P, "layer2": H2 // P, "layer3": 1}
        step_copied = {"turn": turn_copied, "pairs": pairs_copied, "layer1": h1_ready, "layer2": h2_ready,
                       "layer3": y_copied}

        def granule(u, part):
            n = slices[u] // 2
            return range(part * n, (part + 1) * n)

        def raw_table(u):
            return tables[ONE_HOT[u]].rearrange("(p c) d -> p (c d)", p=ROWS)

        def gram_copies(side, r):
            return sum(GRAM_SIDE[n % 4] == side for n in range(r))

        def copy_products(engine, copy, side, pair, slot, r, first):
            if GRAM_SIDE[r % 4] != side:
                return
            engine.wait_ge(gram_done, (pair * 4 + slot) * QBANKS + (r + 1))
            if first and slot == 0 and gram_copies(side, r) == 0:
                engine.wait_ge(lo_ready, NO)
            g = slot * (TILE // QUAD) + 4 * r
            for j in range(QUAD):
                part = slice(j * SLOT, j * SLOT + NODES)
                src = gram_ring[r % 4][part, 0:4 * QUAD * NODES].rearrange("p (w i m) -> p i m w", w=4, i=QUAD)[:, j, :, :]
                ev = copy(products[part, :, g:g + 4], src)
            ev.then_inc(gram_copied[side], 1)

        def for_tiles(pair, hh, last, turn, multiply):
            late = last and hh == 1
            for r in range(QBANKS):
                multiply(2 * hh, r)
                if r < TGROUPS and not late:
                    turn(2 * hh + 1, r)
            if late:
                for q in range(TGROUPS):
                    turn(2 * hh + 1, q)
            for r in range(QBANKS):
                multiply(2 * hh + 1, r)

        block = ctx.enter_context(nc.Block())

        def over_pairs(engine, body):
            body(0, True, False)
            with engine.Fori(1, PAIRS - 1) as pair:
                body(pair, False, False)
            body(PAIRS - 1, False, True)

        @block.sync
        def _(sp):
            def load_ids(half, u):
                sp.dma_start(ids_all[:, u, :], ids_rows[half, u, :].partition_broadcast(P)).then_inc(ids_landed[u], 16)

            def load_dense(tile, slot):
                sp.dma_start(rows[:, slot, 0, :], dense[tile, :, :]).then_inc(dense_landed[slot], 16)

            sp.dma_start(index[:], ids_cols).then_inc(index_landed, 16)
            for u in range(NO):
                sp.dma_start(stage[u][0:SPRAY, :], raw_table(u)[0:SPRAY, :]).then_inc(raw_landed[u], 16)
            for slot in range(2):
                load_dense(slot, slot)
            sp.dma_start(w1d[:], w1[0:D, :]).then_inc(w1d_landed, 16)
            sp.dma_start(dense_t[:], w1[D + NPAIRS:, :]).then_inc(w1d_landed, 16)
            sp.dma_start(w1z[:], w1[D:D + NPAIRS, :].rearrange("(c p) n -> p c n", p=ZROWS)).then_inc(weights_landed, 16)
            sp.dma_start(w2s[:], w2.rearrange("(c p) n -> p c n", p=P)).then_inc(weights_landed, 16)
            sp.dma_start(columns[:], vectors).then_inc(weights_landed, 16)

            sp.wait_ge(lo_ready, NO)
            for slot in range(2, 4):
                load_dense(slot, slot)

            def body(pair, first, last):
                for hh in range(2):
                    half = pair * 2 + hh
                    if not (last and hh == 1):
                        for u in range(NO):
                            sp.wait_ge(one_hot_ready, half * (2 * NO) + 2 * u + 2)
                            load_ids(half + 1, u)
                    if hh == 0:
                        if first:
                            sp.wait_ge(w1d_ready, 1)
                        else:
                            sp.wait_ge(step_done["layer1"], pair * (H1 // P))
                        sp.dma_start(dense_t[:], dense_cols[bass.ds(pair, 1) if not isinstance(pair, int) else slice(pair, pair + 1), :, :]
                                     .rearrange("o d s -> (o d) s")).then_inc(dense_t_landed, 16)
                    if not last:
                        for s in range(2):
                            tile = pair * 4 + (2 * hh + s)
                            sp.wait_ge(rows_turned, tile * TGROUPS + TGROUPS)
                            load_dense(tile + 4, 2 * hh + s)

            over_pairs(sp, body)
            sp.wait_ge(y_copied, PAIRS)
            sp.dma_start(y.rearrange("(q g j) o -> g q (j o)", q=PAIRS, j=QUAD),
                         ys[:].rearrange("g (q j) -> g q j", j=QUAD)).then_inc(y_stored, 16)
            sp.wait_ge(y_stored, 16)

        @block.gpsimd
        def _(pool):
            for kind, n in enumerate((min(slices), max(slices))):
                nc.gpsimd.iota(row_number_i[:, kind, 0:n], [[1, n]], base=0, channel_multiplier=n).then_inc(iota_ready, 1)
            nc.gpsimd.memset(ident[:], 0.0).then_inc(cleared, 1)
            pool.wait_ge(cleared, 1)
            nc.gpsimd.affine_select(out=ident[:], in_=ident[:], compare_op=ALU.not_equal, fill=1.0, base=0,
                                    pattern=[[-1, P]], channel_multiplier=1).then_inc(ident_ready, 1)
            pool.wait_ge(index_landed, 16)

            def body(pair, first, last):
                for slot in range(4):
                    tile = pair * 4 + slot
                    if first and slot == 2:
                        pool.wait_ge(lo_ready, NO)
                    if not first:
                        pool.wait_ge(rows_turned, (tile - 4) * TGROUPS + TGROUPS)
                    nc.gpsimd.tensor_copy(index_now[:, slot, :], index[:, bass.ds(tile * NG, NG)]).then_inc(index_ready, 1)
                    pool.wait_ge(index_ready, tile + 1)
                    nc.gpsimd.tensor_tensor(carrier[:], index_now[:, slot, 0:1], index_now[:, slot, 0:1], ALU.add)
                    for i, f in enumerate(GATHERED):
                        nc.gpsimd.indirect_dma_start(
                            rows[:, slot, 1 + i, :], None, tables[f],
                            bass.IndirectOffsetOnAxis(ap=index_now[:, slot, i:i + 1], axis=0),
                        ).then_inc(rows_landed[slot], 16)

            over_pairs(nc.gpsimd, body)

        @block.tensor
        def _(pe):
            def lookup(pair, hh, u, first):
                half = pair * 2 + hh
                b = (hh * NO + u) % 2
                out = lookup_ps[b][:, 0:HALF]
                if first and hh == 0:
                    pe.wait_ge(hi_ready, u + 1)
                    pe.wait_ge(lo_ready, u + 1)
                if not (first and hh == 0 and u < 2):
                    pe.wait_ge(lookup_copied, half * NO + (u - 1))
                for part in range(2):
                    pe.wait_ge(one_hot_ready, half * (2 * NO) + (2 * u + part + 1))
                    for c in granule(u, part):
                        for table in (part_hi[u], part_lo[u]):
                            mm = nc.tensor.matmul(out, table[:, c, :],
                                                  one_hot[:, (2 * u + part) % ONE_HOT_SLOTS, c - granule(u, part)[0], :],
                                                  start=(c == 0 and table is part_hi[u]),
                                                  stop=(c == slices[u] - 1 and table is part_lo[u]))
                    mm.then_inc(one_hot_used, 1)

            def turn_rows(pair, slot, q, first):
                i = slot * TGROUPS + q
                if q == 0:
                    pe.wait_ge(rows_landed[slot], pair * (16 * NG) + 16 * NG)
                    pe.wait_ge(dense_landed[slot], pair * 16 + 16)
                if not (first and i < 2):
                    pe.wait_ge(rows_copied, pair * (4 * TGROUPS) + (i - 1))
                for n in range(4 * q, min(4 * q + 4, NROWS)):
                    mm = nc.tensor.transpose(rows_ps[i % 2][:, (n % 4) * P:(n % 4 + 1) * P],
                                             rows[:, slot, n, :], ident[:])
                mm.then_inc(rows_turned, 1)

            def products_of(pair, slot, r, first):
                hh, s = divmod(slot, 2)
                if r == 0:
                    pe.wait_ge(rows_copied, pair * (4 * TGROUPS) + (slot + 1) * TGROUPS)
                    if s == 0:
                        pe.wait_ge(lookup_copied, (pair * 2 + hh) * NO + NO)
                if not (first and slot == 0 and r < 4):
                    side = GRAM_SIDE[r % 4]
                    pe.wait_ge(gram_copied[side], (pair * 4 + slot) * gram_copies(side, QBANKS)
                               + (gram_copies(side, r + 1) - gram_copies(side, 4)))
                if slot == 0 and r == 2 and not first:
                    pe.wait_ge(y_copied, pair)
                for w in range(4):
                    c = s * TILE + (4 * r + w) * QUAD
                    mm = nc.tensor.matmul(gram_ring[r % 4][:, w * QUAD * NODES:(w + 1) * QUAD * NODES],
                                          features[:, c:c + QUAD, :], features[:, c:c + QUAD, 0:NODES],
                                          start=True, stop=True)
                mm.then_inc(gram_done, 1)

            def step(pair, kind, n, first):
                i = STEP_AT[kind, n]
                out = mlp_ps[i % 2]
                if i >= 2:
                    bk, bn = STEPS[i - 2]
                    pe.wait_ge(step_copied[bk], pair * per_pair[bk] + (bn + 1))
                if kind == "turn":
                    if n == 0:
                        for side in range(2):
                            n_side = 4 * gram_copies(side, QBANKS)
                            pe.wait_ge(gram_copied[side], pair * n_side + n_side)
                    for m in range(4 * n, min(4 * n + 4, NODES - 1)):
                        mm = nc.tensor.transpose(out[:, (m % 4) * P:(m % 4 + 1) * P], products[:, m, :], ident[:])
                elif kind == "pairs":
                    if n == 0:
                        pe.wait_ge(turn_copied, pair * GTBANKS + GTBANKS)
                    for j in range(QUAD):
                        mm = nc.tensor.transpose(out[0:ZROWS, j * P:(j + 1) * P],
                                                 by_sample[:, j, n * ZROWS:(n + 1) * ZROWS], ident[:])
                elif kind == "layer1":
                    if n == 0:
                        pe.wait_ge(pairs_copied, pair * ZSLICES + ZSLICES)
                        pe.wait_ge(dense_t_landed, pair * 16 + 16)
                        if first:
                            pe.wait_ge(w1d_ready, 1)
                            pe.wait_ge(weights_landed, 48)
                    mm = nc.tensor.matmul(out[:], w1d[:, n * P:(n + 1) * P],
                                          dense_t[:], start=True, stop=False)
                    for c in range(ZSLICES):
                        mm = nc.tensor.matmul(out[:], w1z[:, c, n * P:(n + 1) * P], by_pair[0:ZROWS, c, :],
                                              start=False, stop=(c == ZSLICES - 1))
                elif kind == "layer2":
                    if n == 0:
                        pe.wait_ge(h1_ready, pair * (H1 // P) + H1 // P)
                    for c in range(H1 // P):
                        mm = nc.tensor.matmul(out[:], w2s[:, c, n * P:(n + 1) * P], h1[:, c, :],
                                              start=(c == 0), stop=(c == H1 // P - 1))
                else:
                    pe.wait_ge(h2_ready, pair * (H2 // P) + H2 // P)
                    for j in range(QUAD):
                        for c in range(H2 // P):
                            mm = nc.tensor.matmul(out[:, j:j + 1], h2[:, c, j * GROUPS:(j + 1) * GROUPS],
                                                  w3s[:, c:c + 1], start=(c == 0), stop=(c == H2 // P - 1))
                mm.then_inc(step_done[kind], 1)

            pe.wait_ge(ident_ready, 1)
            pe.wait_ge(padding_ready, 1)

            def body(pair, first, second, last):
                for hh in range(2):
                    for u in range(NO):
                        lookup(pair, hh, u, first)
                        if u >= NO - TGROUPS:
                            turn_rows(pair, 2 * hh, u - (NO - TGROUPS), first)
                        if hh == 0 and not first:
                            for kind, n in AFTER_UNIT[u]:
                                step(pair - 1, kind, n, second)
                    for_tiles(pair, hh, last, lambda slot, q: turn_rows(pair, slot, q, first),
                              lambda slot, r: products_of(pair, slot, r, first))

            body(0, True, False, False)
            body(1, False, True, False)
            with nc.tensor.Fori(2, PAIRS - 1) as pair:
                body(pair, False, False, False)
            body(PAIRS - 1, False, False, True)
            for kind, n in STEPS:
                step(PAIRS - 1, kind, n, False)

        @block.scalar
        def _(act):
            def start_loads(u):
                act.dma_start(ids_all[:, u, :], ids_rows[0, u, :].partition_broadcast(P)).then_inc(ids_landed[u], 16)
                act.dma_start(stage[u][SPRAY:ROWS, :], raw_table(u)[SPRAY:ROWS, :]).then_inc(raw_landed[u], 16)

            def upper_part(u):
                act.wait_ge(raw_landed[u], 32)
                nc.scalar.copy(part_hi[u][:].rearrange("p c d -> p (c d)"), stage[u]).then_inc(hi_ready, 1)

            def copy_rows(pair, slot, q):
                act.wait_ge(rows_turned, (pair * 4 + slot) * TGROUPS + (q + 1))
                n0, n1 = 4 * q, min(4 * q + 4, NROWS)
                s = slot % 2
                nc.scalar.copy(features[:, s * TILE:(s + 1) * TILE, n0:n1],
                               rows_ps[(slot * TGROUPS + q) % 2][:, 0:(n1 - n0) * P].rearrange("p (n b) -> p b n", b=P)
                               ).then_inc(rows_copied, 1)

            start_loads(0)
            for u in range(NO):
                if u + 1 < NO:
                    start_loads(u + 1)
                if u < 2:
                    upper_part(u)

            def step(pair, kind, n, first):
                if kind not in ("pairs", "layer1", "layer2"):
                    return
                src = mlp_ps[STEP_AT[kind, n] % 2]
                act.wait_ge(step_done[kind], pair * per_pair[kind] + (n + 1))
                if kind == "pairs":
                    nc.scalar.copy(by_pair[0:ZROWS, n, :], src[0:ZROWS, :]).then_inc(pairs_copied, 1)
                elif kind == "layer1":
                    if n == 0 and first:
                        act.wait_ge(weights_landed, 48)
                    nc.scalar.activation(h1[:, n, :], src[:], ACT.Relu, bias=b1s[:, n:n + 1]).then_inc(h1_ready, 1)
                else:
                    nc.scalar.activation(h2[:, n, :], src[:], ACT.Relu, bias=b2s[:, n:n + 1]).then_inc(h2_ready, 1)

            def body(pair, first, second, last):
                for hh in range(2):
                    half = pair * 2 + hh
                    for u in range(NO):
                        if first and hh == 0 and u + 2 < NO:
                            upper_part(u + 2)
                        act.wait_ge(one_hot_used, half * (2 * NO) + 2 * u + 2)
                        if first and hh == 0 and u == 0:
                            act.wait_ge(padding_ready, 1)
                        nc.scalar.copy(features[:, :, NROWS + u], lookup_ps[(hh * NO + u) % 2][:, 0:HALF])\
                          .then_inc(lookup_copied, 1)
                        if u >= NO - TGROUPS:
                            copy_rows(pair, 2 * hh, u - (NO - TGROUPS))
                        if hh == 0 and not first:
                            for kind, n in AFTER_UNIT[u]:
                                step(pair - 1, kind, n, second)
                    for_tiles(pair, hh, last, lambda slot, q: copy_rows(pair, slot, q),
                              lambda slot, r: copy_products(act, nc.scalar.copy, 0, pair, slot, r, first))

            body(0, True, False, False)
            body(1, False, True, False)
            with nc.scalar.Fori(2, PAIRS - 1) as pair:
                body(pair, False, False, False)
            body(PAIRS - 1, False, False, True)
            for kind, n in STEPS:
                step(PAIRS - 1, kind, n, False)

        @block.vector
        def _(dve):
            nc.vector.memset(features[:, :, NODES:SLOT], 0.0).then_inc(padding_ready, 1)
            dve.wait_ge(iota_ready, 2)
            for kind, n in enumerate((min(slices), max(slices))):
                nc.vector.tensor_copy(row_number[:, kind, 0:n], row_number_i[:, kind, 0:n])\
                  .then_inc(row_number_ready, 1)

            def split(u):
                dve.wait_ge(raw_landed[u], 32)
                dve.wait_ge(hi_ready, u + 1)
                nc.vector.tensor_tensor(part_lo[u][:].rearrange("p c d -> p (c d)"), stage[u],
                                        part_hi[u][:].rearrange("p c d -> p (c d)").bitcast(F32),
                                        ALU.subtract).then_inc(lo_ready, 1)

            def make_one_hot(half, u, part, wait_used):
                kind = int(slices[u] != min(slices))
                if part == 0:
                    dve.wait_ge(ids_landed[u], half * 16 + 16)
                if wait_used:
                    dve.wait_ge(one_hot_used, half * (2 * NO) + (2 * u + part + 1 - ONE_HOT_SLOTS))
                for c in granule(u, part):
                    ins = nc.vector.tensor_scalar(
                        one_hot[:, (2 * u + part) % ONE_HOT_SLOTS, c - granule(u, part)[0], :],
                        ids_all[0:ROWS, u, :], row_number[0:ROWS, kind, c:c + 1], None, ALU.is_equal)
                ins.then_inc(one_hot_ready, 1)

            dve.wait_ge(row_number_ready, 2)
            for u in range(2):
                split(u)
                for part in range(2):
                    make_one_hot(0, u, part, False)

            def step(pair, kind, n):
                src = mlp_ps[STEP_AT[kind, n] % 2]
                if kind == "turn":
                    dve.wait_ge(step_done[kind], pair * GTBANKS + (n + 1))
                    for m in range(4 * n, min(4 * n + 4, NODES - 1)):
                        ins = nc.vector.tensor_copy(
                            by_sample[:, :, pair_start(m):pair_start(m + 1)],
                            src[:, (m % 4) * P:(m % 4 + 1) * P].rearrange("p (j n) -> p j n", n=SLOT)[:, :, m + 1:NODES])
                    ins.then_inc(turn_copied, 1)
                elif kind == "layer3":
                    dve.wait_ge(step_done[kind], pair + 1)
                    nc.vector.tensor_copy(ys[:, bass.ds(pair * QUAD, QUAD)], src[:, 0:QUAD]).then_inc(y_copied, 1)

            def body(pair, first, last):
                for hh in range(2):
                    half = pair * 2 + hh
                    for u in range(NO):
                        if u + 2 < NO:
                            if first and hh == 0:
                                split(u + 2)
                            make_one_hot(half, u + 2, 0, True)
                        if hh == 0 and not first:
                            for kind, n in AFTER_UNIT[u]:
                                step(pair - 1, kind, n)
                        if u + 2 < NO:
                            make_one_hot(half, u + 2, 1, True)
                    if first and hh == 0:
                        dve.wait_ge(w1d_landed, 32)
                        nc.vector.tensor_tensor(w1d[:], w1d[:], dense_t[:], ALU.add).then_inc(w1d_ready, 1)

                    def multiply(slot, r):
                        copy_products(dve, nc.vector.tensor_copy, 1, pair, slot, r, first)
                        if slot % 2 == 1 and r in (1, 3, 5, 7) and not (last and hh == 1):
                            make_one_hot(half + 1, (r // 2) // 2, (r // 2) % 2, True)

                    for_tiles(pair, hh, last, lambda slot, q: None,
                              multiply)

            over_pairs(nc.vector, body)
            for kind, n in STEPS:
                step(PAIRS - 1, kind, n)


def kernel(**inputs):
    import concourse.bacc as bacc
    from concourse.bass_utils import run_bass_kernel_spmd

    nc = bacc.Bacc("TRN2", target_bir_lowering=False, num_devices=1)
    arrays = {}

    def given(name, a):
        a = np.ascontiguousarray(a)
        arrays[f"in_{name}"] = a
        return nc.dram_tensor(f"in_{name}", a.shape, mybir.dt.from_np(a.dtype), kind="ExternalInput").ap()

    ids = np.asarray(inputs["ids"])
    w1 = np.asarray(inputs["W_top1"])
    place = {}
    for a in range(NODES):
        for b in range(a + 1, NODES):
            place[a, b] = D + pair_start(a) + b - a - 1
    pair_rows = [place[min(ORDER[a], ORDER[b]), max(ORDER[a], ORDER[b])]
                 for a in range(NODES) for b in range(a + 1, NODES)]
    w1_order = list(range(D)) + pair_rows + list(range(D + NPAIRS, 2 * D + NPAIRS))
    build(
        nc,
        given("dense", np.asarray(inputs["r_dense_features"]).reshape(TILES, TILE, D)),
        given("dense_cols", np.asarray(inputs["r_dense_features"]).reshape(PAIRS, GROUPS, QUAD, D)
              .transpose(0, 3, 2, 1).reshape(PAIRS, D, PAIR)),
        given("ids_rows", ids[:, ONE_HOT].reshape(HALVES, HALF, NO).transpose(0, 2, 1)),
        given("ids_cols", ids[:, GATHERED].reshape(TILES, TILE, NG).transpose(1, 0, 2).reshape(TILE, TILES * NG)),
        [given(f"tbl_{f}", inputs[f"tbl_{f}"]) for f in range(TABLES)],
        given("w1", w1[w1_order]),
        given("w2", inputs["W_top2"]),
        given("vectors", np.concatenate([np.asarray(inputs[n]).reshape(-1, P).T
                                         for n in ("b_top1", "b_top2", "W_top3")], axis=1)),
        nc.dram_tensor("out_y", (B, 1), F32, kind="ExternalOutput").ap(),
    )
    return run_bass_kernel_spmd(nc, [arrays], core_ids=[0]).results[0]["out_y"]
```

```python
from contextlib import ExitStack

import numpy as np

import concourse.bass as bass
from concourse import mybir

ALU = mybir.AluOpType
ACT = mybir.ActivationFunctionType
F32 = mybir.dt.float32
F32R = mybir.dt.float32r
I32 = mybir.dt.int32

B, D, TABLES = 2048, 128, 26
NODES = TABLES + 1
P = 128
TILE = 128
GROUP = 2 * TILE
TILES, GROUPS = B // TILE, B // GROUP
RING = 4
QUAD = 4
SLOT = P // QUAD
PAD = SLOT - NODES
BLOCK = 32
BLOCKS = GROUP // QUAD // BLOCK
NPAIRS = NODES * (NODES - 1) // 2
ZSPLIT = [0, 5, 11, 26]
ZSLICES = len(ZSPLIT) - 1
H1, H2 = 512, 256
ROWS = 125
SPRAY = 112

ONE_HOT = [5, 7, 9, 11, 13, 20, 25]
GATHERED = [f for f in range(TABLES) if f not in ONE_HOT]
NG, NO = len(GATHERED), len(ONE_HOT)
ORDER = [0] + [1 + f for f in GATHERED] + [1 + f for f in ONE_HOT]
TGROUPS = -(-NG // 4)
QBANKS = TILE // QUAD // 4
GRAM_SIDE = [0, 1, 0, 0]
MAXSLICE = 4
ONE_HOT_SLOTS = 7
ONE_HOT_BESIDE = [2, 3, 4, 6, 7, 8, 9]
TURN_BESIDE = 10


def pair_start(n):
    return n * (2 * NODES - n - 1) // 2


ZROWS = [pair_start(b) - pair_start(a) for a, b in zip(ZSPLIT, ZSPLIT[1:])]
ZAT = [sum(ZROWS[:c]) + sum(PAD + n + 1 for n in ZSPLIT[:c + 1]) for c in range(ZSLICES)]
_last = [(n, 2) for n in reversed(range(ZSPLIT[2], ZSPLIT[3]))]
_rest = [(n, c) for pair in zip(reversed(range(ZSPLIT[0], ZSPLIT[1])), reversed(range(ZSPLIT[1] + 1, ZSPLIT[2])))
         for c, n in enumerate(pair)] + [(ZSPLIT[1], 1)]
TURN_ORDER = [x for i, last in enumerate(_last) for x in [last] + _rest[i:i + 1]]

STEPS = ([("pairs", c) for c in range(ZSLICES)] + [("layer1", m) for m in range(H1 // P)]
         + [("layer2", m) for m in range(H2 // P)] + [("layer3", 0)])
STEP_AT = {step: i for i, step in enumerate(STEPS)}
TURNS = [("rows", q) for q in range(TGROUPS)]
AFTER_UNIT = {2: STEPS[0:2] + TURNS[0:1] + STEPS[2:3], 3: STEPS[3:5], 4: TURNS[1:2] + STEPS[5:6],
              5: STEPS[6:7] + TURNS[2:4] + STEPS[7:9], 6: TURNS[4:5] + STEPS[9:10]}
AFTER_UNIT_AT_START = [{5: TURNS[0:4], 6: TURNS[4:5]},
                       {5: STEPS[0:3], 6: STEPS[3:7] + TURNS[0:1] + STEPS[7:9] + TURNS[1:5] + STEPS[9:10]}]
EARLY = 4
EARLY_FIRST, EARLY_BESIDE = range(5), {2: [5], 3: [6], 7: [7], 8: range(8, 14)}
SPLIT_AFTER = {1: [0], 5: [1], 6: [2], 7: [3], 9: [4], 11: [5], 13: [6]}
SPLIT_AHEAD = 3
ACT_TAILS = 2
TURNED_BY = [1 + max(i for i, (_, c) in enumerate(TURN_ORDER) if c == slice_c) for slice_c in range(ZSLICES)]


def build(nc, dense_cols, ids_rows, ids_cols, tables, w1, w2, vectors, y):
    slices = [tables[f].shape[0] // ROWS for f in ONE_HOT]
    assert all(tables[f].shape[0] == ROWS * slices[0] for f in ONE_HOT)
    assert all(sorted(sum(after.values(), [])) == sorted(STEPS + TURNS) for after in (AFTER_UNIT, AFTER_UNIT_AT_START[1]))
    assert sum(ZROWS) == NPAIRS and max(ZROWS) <= P and len(STEPS) % 2 == 0 and len(TURN_ORDER) == NODES - 1

    with ExitStack() as ctx:
        def sb(name, shape, dt=F32):
            return ctx.enter_context(nc.sbuf_tensor(name, shape, dt))

        def bank(name):
            return ctx.enter_context(nc.psum_tensor(name, [P, 512], F32))

        def sem(name):
            return ctx.enter_context(nc.semaphore(name))

        ident = sb("ident", [P, P])
        row_number_i = sb("row_number_i", [P, slices[0]], I32)
        row_number = sb("row_number", [P, slices[0]])
        index = sb("index", [P, TILES * NG], I32)
        index_now = sb("index_now", [P, RING, NG], I32)
        w1d = sb("w1d", [P, H1])
        w1z = sb("w1z", [P, ZSLICES, H1])
        w2s = sb("w2s", [P, H1 // P, H2])
        columns = sb("columns", [P, (H1 + 2 * H2) // P])
        b1s, b2s, w3s = (columns[:, a // P:b // P] for a, b in ((0, H1), (H1, H1 + H2), (H1 + H2, H1 + 2 * H2)))
        part_hi = [sb(f"part_hi{u}", [ROWS, n, D], F32R) for u, n in enumerate(slices)]
        part_lo = [sb(f"part_lo{u}", [ROWS, n, D], F32R) for u, n in enumerate(slices)]
        carrier = sb("carrier", [P, 1], I32)
        warm = sb("warm", [P, 1])
        rows = sb("rows", [P, RING, NG, D])
        ids_all = sb("ids_all", [P, NO, GROUP], I32)
        one_hot = sb("one_hot", [ROWS, ONE_HOT_SLOTS, MAXSLICE, GROUP], F32R)
        features = sb("features", [P, GROUP, SLOT])
        dense_t = sb("dense_t", [P, 2, GROUP])
        y_row = sb("y_row", [1, GROUP])
        widths = [(NODES - 1) * (GROUP // QUAD), BLOCKS * (ZAT[-1] + ZROWS[-1]), ZSLICES * GROUP]
        work = sb("work", [P, sum(widths)])
        products, by_sample, by_pair = (work[:, sum(widths[:i]):sum(widths[:i + 1])] for i in range(3))
        h1 = products[:, 0:H1 // P * GROUP].rearrange("p (m s) -> p m s", s=GROUP)
        h2 = products[:, H1 // P * GROUP:(H1 + H2) // P * GROUP].rearrange("p (m s) -> p m s", s=GROUP)
        products = products.rearrange("p (n g) -> p n g", g=GROUP // QUAD)
        by_sample = by_sample.rearrange("p (b n) -> p b n", b=BLOCKS)
        by_pair = by_pair.rearrange("p (c s) -> p c s", s=GROUP)
        late_rows = [rows[:, slot, :, :].rearrange("p n d -> p (n d)") for slot in (2, 3)]
        at = [sum(slices[:u]) * D for u in range(4)]
        stage = [area[0:ROWS, a:a + n * D] for n, (area, a) in zip(slices, (
            (work, at[0]), (work, at[1]), (work, at[2]), (late_rows[0], 0), (late_rows[0], slices[3] * D),
            (late_rows[1], 0), (late_rows[1], slices[5] * D)))]
        assert at[3] <= sum(widths)

        rows_ps = [bank(f"rows_ps{i}") for i in range(2)]
        lookup_ps = [bank(f"lookup_ps{i}") for i in range(2)]
        gram_ps = [bank(f"gram_ps{i}") for i in range(2)]
        mlp_ps = [bank(f"mlp_ps{i}") for i in range(2)]
        gram_ring = gram_ps + mlp_ps
        last_layer1 = lookup_ps + mlp_ps
        last_pairs = rows_ps + gram_ps[0:1]
        last_layer2 = rows_ps
        last_layer3 = gram_ps[1]

        index_landed = sem("index_landed")
        raw_landed = [sem(f"raw_landed{u}") for u in range(NO)]
        ids_0_landed, ids_others_landed = sem("ids_0_landed"), sem("ids_others_landed")
        ids_landed = [sem(f"ids_landed{u}") for u in range(NO)]
        rows_landed = [sem(f"rows_landed{i}") for i in range(RING)]
        w1d_landed = sem("w1d_landed")
        dense_t_landed = [sem(f"dense_t_landed{i}") for i in range(2)]
        weights_landed = sem("weights_landed")
        y_stored = sem("y_stored")
        cleared = sem("cleared")
        ident_ready = sem("ident_ready")
        iota_ready = sem("iota_ready")
        index_ready = sem("index_ready")
        row_number_ready = sem("row_number_ready")
        padding_ready = sem("padding_ready")
        lo_ready = sem("lo_ready")
        w1d_ready = sem("w1d_ready")
        one_hot_ready = sem("one_hot_ready")
        products_turned = sem("products_turned")
        y_copied = sem("y_copied")
        hi_ready = sem("hi_ready")
        lookup_copied = sem("lookup_copied")
        dense_copied = sem("dense_copied")
        pairs_copied = sem("pairs_copied")
        h1_ready = sem("h1_ready")
        h2_ready = sem("h2_ready")
        rows_copied = sem("rows_copied")
        gram_copied = [sem("gram_copied_act"), sem("gram_copied_dve")]
        one_hot_used = sem("one_hot_used")
        rows_turned = sem("rows_turned")
        gram_done = sem("gram_done")
        step_done = {kind: sem(f"{kind}_done") for kind in ("pairs", "layer1", "layer2", "layer3")}
        per_group = {"pairs": ZSLICES, "layer1": H1 // P, "layer2": H2 // P, "layer3": 1}
        step_copied = {"pairs": pairs_copied, "layer1": h1_ready, "layer2": h2_ready,
                       "layer3": y_copied}

        granules = []
        for u, n in enumerate(slices):
            parts = 2 * -(-n // (2 * MAXSLICE))
            granules += [(u, part.tolist()) for part in np.array_split(np.arange(n), parts)]
        NGRAN = len(granules)
        used_by = [sum(v <= u for v, _ in granules) for u in range(NO)]
        assert NGRAN % ONE_HOT_SLOTS == 0 and len(ONE_HOT_BESIDE) == ONE_HOT_SLOTS

        def load_tail(engine, u):
            engine.dma_start(stage[u][SPRAY:ROWS, :], raw_table(u)[SPRAY:ROWS, :]).then_inc(raw_landed[u], 16)

        def raw_table(u):
            return tables[ONE_HOT[u]].rearrange("(p c) d -> p (c d)", p=ROWS)

        def gram_copies(side, r):
            return sum(GRAM_SIDE[n % 4] == side for n in range(r))

        def lookup_columns(odd, u):
            at = u // 2 % 2 * GROUP
            return lookup_ps[(odd * NO + u) % 2][:, at:at + GROUP]

        def copy_products(engine, copy, side, group, s, r, first):
            if GRAM_SIDE[r % 4] != side:
                return
            engine.wait_ge(gram_done, (group * 2 + s) * QBANKS + (r + 1))
            if first and s == 0 and gram_copies(side, r) == 0:
                engine.wait_ge(lo_ready, NO)
            g = s * (TILE // QUAD) + 4 * r
            for j in range(QUAD):
                part = slice(j * SLOT, (j + 1) * SLOT)
                src = gram_ring[r % 4][part, 0:4 * QUAD * (NODES - 1)].rearrange("p (w i m) -> p i m w", w=4, i=QUAD)[:, j, :, :]
                ev = copy(products[part, :, g:g + 4], src)
            ev.then_inc(gram_copied[side], 1)

        def for_tiles(late, turn_bank, multiply, between=lambda: None):
            for r in range(QBANKS):
                multiply(0, r)
                if r < TGROUPS and not late:
                    turn_bank(1, r)
            between()
            if late:
                for q in range(TGROUPS):
                    turn_bank(1, q)
            for r in range(QBANKS):
                multiply(1, r)

        def at_start(turn):
            return type(turn) is int and turn == 0

        def after_unit(u, turn, odd):
            return (AFTER_UNIT_AT_START[odd] if at_start(turn) else AFTER_UNIT).get(u, [])

        def early(turn, odd):
            return EARLY if at_start(turn) and odd else 0

        block = ctx.enter_context(nc.Block())

        def over_groups(engine, body):
            body(0, 0, True, False)
            body(0, 1, False, False)
            with engine.Fori(1, GROUPS // 2 - 1) as turn:
                body(turn, 0, False, False)
                body(turn, 1, False, False)
            body(GROUPS // 2 - 1, 0, False, False)
            body(GROUPS // 2 - 1, 1, False, True)

        @block.sync
        def _(sp):
            def load_ids(group, u):
                sp.dma_start(ids_all[:, u, :], ids_rows[group, u, :].partition_broadcast(P)).then_inc(ids_landed[u], 16)

            def load_dense(group, odd):
                sp.dma_start(dense_t[:, odd, :], dense_cols[:, bass.ds(group * GROUP, GROUP)]).then_inc(dense_t_landed[odd], 16)

            def store_y(group):
                sp.wait_ge(y_copied, group + 1)
                sp.dma_start(y[bass.ds(group * GROUP, GROUP), :].rearrange("(a s) o -> a (s o)", a=1), y_row[:]
                             ).then_inc(y_stored, 16)

            sp.dma_start(index[:], ids_cols).then_inc(index_landed, 16)
            for u in range(NO):
                sp.dma_start(stage[u][0:SPRAY, :], raw_table(u)[0:SPRAY, :]).then_inc(raw_landed[u], 16)
                if u == 0:
                    sp.dma_start(ids_all[:, 1:NO, :].rearrange("p u s -> p (u s)"),
                                 ids_rows[0, 1:NO, :].rearrange("u s -> (u s)").partition_broadcast(P)
                                 ).then_inc(ids_others_landed, 16)
                if u >= ACT_TAILS:
                    load_tail(sp, u)
            sp.dma_start(w1d[:], w1[0:D, :]).then_inc(w1d_landed, 16)
            sp.dma_start(dense_t[:].rearrange("p i s -> p (i s)"), w1[D + NPAIRS:, :]).then_inc(w1d_landed, 16)
            for c in range(ZSLICES):
                at = D + sum(ZROWS[:c])
                sp.dma_start(w1z[0:ZROWS[c], c, :], w1[at:at + ZROWS[c], :]).then_inc(weights_landed, 16)
            sp.dma_start(w2s[:], w2.rearrange("(c p) n -> p c n", p=P)).then_inc(weights_landed, 16)
            sp.dma_start(columns[:], vectors).then_inc(weights_landed, 16)

            def body(turn, odd, first, last):
                group = turn * 2 + odd
                if not last:
                    for u in range(NO):
                        sp.wait_ge(one_hot_ready, group * NGRAN + used_by[u])
                        load_ids(group + 1, u)
                        if first and u == NO - 1:
                            sp.wait_ge(w1d_ready, 1)
                            load_dense(0, 0)
                            load_dense(1, 1)
                if not first:
                    if not last:
                        sp.wait_ge(step_done["layer1"], group * (H1 // P))
                        load_dense(group + 1, 1 - odd)
                    store_y(group - 1)

            over_groups(sp, body)
            store_y(GROUPS - 1)
            sp.wait_ge(y_stored, GROUPS * 16)

        @block.gpsimd
        def _(pool):
            nc.gpsimd.iota(row_number_i[:], [[1, slices[0]]], base=0, channel_multiplier=slices[0]).then_inc(iota_ready, 1)
            nc.gpsimd.memset(ident[:], 0.0).then_inc(cleared, 1)
            pool.wait_ge(cleared, 1)
            nc.gpsimd.affine_select(out=ident[:], in_=ident[:], compare_op=ALU.not_equal, fill=1.0, base=0,
                                    pattern=[[-1, P]], channel_multiplier=1).then_inc(ident_ready, 1)
            pool.wait_ge(index_landed, 16)

            def body(turn, first):
                for slot in range(RING):
                    tile = turn * RING + slot
                    if first and slot == 2:
                        pool.wait_ge(lo_ready, NO)
                    if not first:
                        pool.wait_ge(rows_turned, (tile - RING) * TGROUPS + TGROUPS)
                    nc.gpsimd.tensor_copy(index_now[:, slot, :], index[:, bass.ds(tile * NG, NG)]).then_inc(index_ready, 1)
                    pool.wait_ge(index_ready, tile + 1)
                    nc.gpsimd.tensor_tensor(carrier[:], index_now[:, slot, 0:1], index_now[:, slot, 0:1], ALU.add)
                    for i, f in enumerate(GATHERED):
                        nc.gpsimd.indirect_dma_start(
                            rows[:, slot, i, :], None, tables[f],
                            bass.IndirectOffsetOnAxis(ap=index_now[:, slot, i:i + 1], axis=0),
                        ).then_inc(rows_landed[slot], 16)

            body(0, True)
            with nc.gpsimd.Fori(1, TILES // RING) as turn:
                body(turn, False)

        @block.tensor
        def _(pe):
            def lookup(group, odd, u, first, early=False):
                out = lookup_columns(odd, u)
                if first:
                    pe.wait_ge(hi_ready, u + 1)
                    pe.wait_ge(lo_ready, u + 1)
                if early:
                    pe.wait_ge(lookup_copied, group * NO)
                elif not (first and u < 2):
                    pe.wait_ge(lookup_copied, group * NO + (u - 1))
                for g, (v, part) in enumerate(granules):
                    if v != u:
                        continue
                    pe.wait_ge(one_hot_ready, group * NGRAN + (g + 1))
                    for c in part:
                        for table in (part_hi[u], part_lo[u]):
                            mm = nc.tensor.matmul(out, table[:, c, :], one_hot[:, g % ONE_HOT_SLOTS, c - part[0], :],
                                                  start=(c == 0 and table is part_hi[u]),
                                                  stop=(c == slices[u] - 1 and table is part_lo[u]))
                    mm.then_inc(one_hot_used, 1)

            def turn_rows(turn, odd, s, q, first):
                tile, slot = (turn * 2 + odd) * 2 + s, 2 * odd + s
                if q == 0:
                    pe.wait_ge(rows_landed[slot], turn * (16 * NG) + 16 * NG)
                if not (first and s == 0 and q < 2):
                    pe.wait_ge(rows_copied, tile * TGROUPS + (q - 1))
                for n in range(4 * q, min(4 * q + 4, NG)):
                    mm = nc.tensor.transpose(rows_ps[(s * TGROUPS + q) % 2][:, (n % 4) * P:(n % 4 + 1) * P],
                                             rows[:, slot, n, :], ident[:])
                mm.then_inc(rows_turned, 1)

            def products_of(group, s, r, first):
                tile = group * 2 + s
                if r == 0:
                    pe.wait_ge(rows_copied, tile * TGROUPS + TGROUPS)
                    if s == 0:
                        pe.wait_ge(lookup_copied, group * NO + NO)
                        pe.wait_ge(dense_copied, group + 1)
                if not (first and s == 0 and r < 4):
                    side = GRAM_SIDE[r % 4]
                    pe.wait_ge(gram_copied[side], tile * gram_copies(side, QBANKS)
                               + (gram_copies(side, r + 1) - gram_copies(side, 4)))
                if s == 0 and r == 3 and not first:
                    pe.wait_ge(y_copied, group)
                for w in range(4):
                    c = s * TILE + (4 * r + w) * QUAD
                    mm = nc.tensor.matmul(gram_ring[r % 4][:, w * QUAD * (NODES - 1):(w + 1) * QUAD * (NODES - 1)],
                                          features[:, c:c + QUAD, :], features[:, c:c + QUAD, PAD:SLOT - 1],
                                          start=True, stop=True)
                mm.then_inc(gram_done, 1)

            def step(turn, odd, kind, n, first):
                group = turn * 2 + odd
                i = STEP_AT[kind, n]
                out = mlp_ps[i % 2][:, 0:GROUP]
                if i >= 2:
                    bk, bn = STEPS[i - 2]
                    pe.wait_ge(step_copied[bk], group * per_group[bk] + (bn + 1))
                if kind == "pairs":
                    pe.wait_ge(products_turned, (group * 2 + 1) * (NODES - 1) + TURNED_BY[n])
                    for b in range(BLOCKS):
                        mm = nc.tensor.transpose(out[0:ZROWS[n], b * P:(b + 1) * P],
                                                 by_sample[:, b, ZAT[n]:ZAT[n] + ZROWS[n]], ident[:])
                elif kind == "layer1":
                    if n == 0:
                        pe.wait_ge(pairs_copied, group * ZSLICES + ZSLICES)
                        pe.wait_ge(dense_t_landed[odd], turn * 16 + 16)
                        if first:
                            pe.wait_ge(w1d_ready, 1)
                            pe.wait_ge(weights_landed, 16 * (ZSLICES + 2))
                    mm = nc.tensor.matmul(out, w1d[:, n * P:(n + 1) * P], dense_t[:, odd, :], start=True, stop=False)
                    for c in range(ZSLICES):
                        mm = nc.tensor.matmul(out, w1z[0:ZROWS[c], c, n * P:(n + 1) * P], by_pair[0:ZROWS[c], c, :],
                                              start=False, stop=(c == ZSLICES - 1))
                elif kind == "layer2":
                    if n == 0:
                        pe.wait_ge(h1_ready, group * (H1 // P) + H1 // P)
                    for c in range(H1 // P):
                        mm = nc.tensor.matmul(out, w2s[:, c, n * P:(n + 1) * P], h1[:, c, :],
                                              start=(c == 0), stop=(c == H1 // P - 1))
                else:
                    pe.wait_ge(h2_ready, group * (H2 // P) + H2 // P)
                    for c in range(H2 // P):
                        mm = nc.tensor.matmul(out[0:1, :], w3s[:, c:c + 1], h2[:, c, :],
                                              start=(c == 0), stop=(c == H2 // P - 1))
                mm.then_inc(step_done[kind], 1)

            def look_up_early(first):
                if first:
                    for u in range(EARLY):
                        lookup(1, 1, u, False, True)

            pe.wait_ge(ident_ready, 1)
            pe.wait_ge(padding_ready, 1)

            def body(turn, odd, first, last):
                group = turn * 2 + odd
                for u in range(NO):
                    if u >= early(turn, odd):
                        lookup(group, odd, u, first)
                    for kind, n in after_unit(u, turn, odd):
                        if kind == "rows":
                            turn_rows(turn, odd, 0, n, first)
                        else:
                            step(turn + odd - 1, 1 - odd, kind, n, at_start(turn))
                for_tiles(at_start(turn) or last,
                          lambda s, q: turn_rows(turn, odd, s, q, first),
                          lambda s, r: products_of(group, s, r, first),
                          lambda: look_up_early(first))

            over_groups(nc.tensor, body)

            group = GROUPS - 1
            for m in range(H1 // P):
                if last_layer1[m] is gram_ring[2]:
                    for side in range(2):
                        pe.wait_ge(gram_copied[side], TILES * gram_copies(side, QBANKS))
                nc.tensor.matmul(last_layer1[m][:, 0:GROUP], w1d[:, m * P:(m + 1) * P], dense_t[:, 1, :], start=True, stop=False)
            for c in range(ZSLICES):
                pe.wait_ge(products_turned, (TILES - 1) * (NODES - 1) + TURNED_BY[c])
                for b in range(BLOCKS):
                    mm = nc.tensor.transpose(last_pairs[c][0:ZROWS[c], b * P:(b + 1) * P],
                                             by_sample[:, b, ZAT[c]:ZAT[c] + ZROWS[c]], ident[:])
                mm.then_inc(step_done["pairs"], 1)
            for c in range(ZSLICES):
                pe.wait_ge(pairs_copied, group * ZSLICES + (c + 1))
                for m in range(H1 // P):
                    mm = nc.tensor.matmul(last_layer1[m][:, 0:GROUP], w1z[0:ZROWS[c], c, m * P:(m + 1) * P],
                                          by_pair[0:ZROWS[c], c, :], start=False, stop=(c == ZSLICES - 1))
                    if c == ZSLICES - 1:
                        mm.then_inc(step_done["layer1"], 1)
            for c in range(H1 // P):
                pe.wait_ge(h1_ready, group * (H1 // P) + (c + 1))
                for m in range(H2 // P):
                    mm = nc.tensor.matmul(last_layer2[m][:, 0:GROUP], w2s[:, c, m * P:(m + 1) * P], h1[:, c, :],
                                          start=(c == 0), stop=(c == H1 // P - 1))
                    if c == H1 // P - 1:
                        mm.then_inc(step_done["layer2"], 1)
            for c in range(H2 // P):
                pe.wait_ge(h2_ready, group * (H2 // P) + (c + 1))
                mm = nc.tensor.matmul(last_layer3[0:1, 0:GROUP], w3s[:, c:c + 1], h2[:, c, :],
                                      start=(c == 0), stop=(c == H2 // P - 1))
            mm.then_inc(step_done["layer3"], 1)

        @block.scalar
        def _(act):
            def upper_part(u):
                act.wait_ge(raw_landed[u], 32)
                nc.scalar.copy(part_hi[u][:].rearrange("p c d -> p (c d)"), stage[u]).then_inc(hi_ready, 1)

            def copy_rows(group, s, q):
                act.wait_ge(rows_turned, (group * 2 + s) * TGROUPS + (q + 1))
                n0, n1 = 4 * q, min(4 * q + 4, NG)
                nc.scalar.copy(features[:, s * TILE:(s + 1) * TILE, PAD + 1 + n0:PAD + 1 + n1],
                               rows_ps[(s * TGROUPS + q) % 2][:, 0:(n1 - n0) * P].rearrange("p (n b) -> p b n", b=P)
                               ).then_inc(rows_copied, 1)

            act.dma_start(ids_all[:, 0, :], ids_rows[0, 0, :].partition_broadcast(P)).then_inc(ids_0_landed, 16)
            for u in range(ACT_TAILS):
                load_tail(act, u)
            act.wait_ge(padding_ready, 1)
            nc.scalar.activation(warm[:], features[:, 0, 0:1], ACT.Relu)
            for u in range(SPLIT_AHEAD):
                upper_part(u)

            def step(group, kind, n, first, banks):
                if kind == "layer3":
                    return
                src = (banks[n] if banks else mlp_ps[STEP_AT[kind, n] % 2])[:, 0:GROUP]
                act.wait_ge(step_done[kind], group * per_group[kind] + (n + 1))
                if kind == "pairs":
                    nc.scalar.copy(by_pair[0:ZROWS[n], n, :], src[0:ZROWS[n], :]).then_inc(pairs_copied, 1)
                elif kind == "layer1":
                    if n == 0 and first:
                        act.wait_ge(weights_landed, 16 * (ZSLICES + 2))
                    nc.scalar.activation(h1[:, n, :], src, ACT.Relu, bias=b1s[:, n:n + 1]).then_inc(h1_ready, 1)
                else:
                    nc.scalar.activation(h2[:, n, :], src, ACT.Relu, bias=b2s[:, n:n + 1]).then_inc(h2_ready, 1)

            def body(turn, odd, first, last):
                group = turn * 2 + odd
                for u in range(NO):
                    if u == 0 and early(turn, odd):
                        act.wait_ge(gram_done, group * (2 * QBANKS))
                    act.wait_ge(one_hot_used, group * NGRAN + used_by[u])
                    nc.scalar.copy(features[:, :, PAD + 1 + NG + u], lookup_columns(odd, u))\
                      .then_inc(lookup_copied, 1)
                    if first and u + SPLIT_AHEAD < NO:
                        upper_part(u + SPLIT_AHEAD)
                    for kind, n in after_unit(u, turn, odd):
                        if kind == "rows":
                            copy_rows(group, 0, n)
                        else:
                            step(group - 1, kind, n, at_start(turn), None)
                    if u == NO - 2:
                        act.wait_ge(dense_t_landed[odd], turn * 16 + 16)
                        nc.scalar.copy(features[:, :, PAD].rearrange("p (b g j) -> p b j g", b=BLOCKS, j=QUAD),
                                       dense_t[:, odd, :].rearrange("p (b j g) -> p b j g", j=QUAD, g=BLOCK)
                                       ).then_inc(dense_copied, 1)
                for_tiles(at_start(turn) or last, lambda s, q: copy_rows(group, s, q),
                          lambda s, r: copy_products(act, nc.scalar.copy, 0, group, s, r, first))

            over_groups(nc.scalar, body)
            for kind, banks in (("pairs", last_pairs), ("layer1", last_layer1), ("layer2", last_layer2)):
                for n in range(len(banks)):
                    step(GROUPS - 1, kind, n, False, banks)

        @block.vector
        def _(dve):
            nc.vector.memset(features[:, :, 0:PAD], 0.0).then_inc(padding_ready, 1)
            dve.wait_ge(iota_ready, 1)
            nc.vector.tensor_copy(row_number[:], row_number_i[:]).then_inc(row_number_ready, 1)

            def split(u):
                dve.wait_ge(raw_landed[u], 32)
                dve.wait_ge(hi_ready, u + 1)
                nc.vector.tensor_tensor(part_lo[u][:].rearrange("p c d -> p (c d)"), stage[u],
                                        part_hi[u][:].rearrange("p c d -> p (c d)").bitcast(F32),
                                        ALU.subtract).then_inc(lo_ready, 1)

            def split_after(g):
                for u in SPLIT_AFTER.get(g, []):
                    split(u)

            def make_one_hot(group, g, very_first):
                u, part = granules[g]
                if very_first:
                    dve.wait_ge(ids_0_landed if u == 0 else ids_others_landed, 16)
                elif part[0] == 0:
                    dve.wait_ge(ids_landed[u], group * 16)
                if not very_first or g >= ONE_HOT_SLOTS:
                    dve.wait_ge(one_hot_used, group * NGRAN + (g + 1 - ONE_HOT_SLOTS))
                for c in part:
                    ins = nc.vector.tensor_scalar(one_hot[:, g % ONE_HOT_SLOTS, c - part[0], :], ids_all[0:ROWS, u, :],
                                                  row_number[0:ROWS, c:c + 1], None, ALU.is_equal)
                ins.then_inc(one_hot_ready, 1)

            dve.wait_ge(row_number_ready, 1)
            for g in range(ONE_HOT_SLOTS):
                make_one_hot(0, g, True)
                split_after(g)

            def turn_products(group, s):
                tile = group * 2 + s
                for side in range(2):
                    n_tile = gram_copies(side, QBANKS)
                    dve.wait_ge(gram_copied[side], tile * n_tile + n_tile)
                for n, c in TURN_ORDER:
                    if n + 1 < ZSPLIT[c + 1]:
                        dve.wait_ge(products_turned, tile * (NODES - 1) + (TURN_ORDER.index((n + 1, c)) + 1))
                    at = ZAT[c] + pair_start(n) - pair_start(ZSPLIT[c]) - (PAD + n + 1)
                    nc.vector.transpose(by_sample[:, s, at:at + SLOT], products[:, n, s * BLOCK:(s + 1) * BLOCK]
                                        ).then_inc(products_turned, 1)

            def copy_y(group, src, first):
                dve.wait_ge(step_done["layer3"], group + 1)
                if not first:
                    dve.wait_ge(y_stored, group * 16)
                nc.vector.tensor_copy(y_row[:].rearrange("p (b g j) -> p b j g", g=BLOCK, j=QUAD),
                                      src[0:1, 0:GROUP].rearrange("p (b j g) -> p b j g", j=QUAD, g=BLOCK)).then_inc(y_copied, 1)

            def body(turn, odd, first, last):
                group = turn * 2 + odd
                if not first:
                    turn_products(group - 1, 1)
                for g in range(ONE_HOT_SLOTS, 0 if early(turn, odd) else NGRAN):
                    make_one_hot(group, g, first)
                    if first:
                        split_after(g)
                if first:
                    dve.wait_ge(w1d_landed, 32)
                    nc.vector.tensor_tensor(w1d[:], w1d[:], dense_t[:].rearrange("p i s -> p (i s)"), ALU.add).then_inc(w1d_ready, 1)
                    for g in EARLY_FIRST:
                        make_one_hot(1, g, False)
                else:
                    copy_y(group - 1, mlp_ps[STEP_AT["layer3", 0] % 2], at_start(turn))

                def multiply(s, r):
                    beside = s * QBANKS + r
                    if first:
                        for g in EARLY_BESIDE.get(beside, []):
                            make_one_hot(1, g, False)
                    if beside in ONE_HOT_BESIDE and not first and not last:
                        make_one_hot(group + 1, ONE_HOT_BESIDE.index(beside), False)
                    if beside == TURN_BESIDE:
                        turn_products(group, 0)
                    copy_products(dve, nc.vector.tensor_copy, 1, group, s, r, first)

                for_tiles(at_start(turn) or last, lambda s, q: None, multiply)

            over_groups(nc.vector, body)
            turn_products(GROUPS - 1, 1)
            copy_y(GROUPS - 1, last_layer3, False)


def kernel(**inputs):
    import concourse.bacc as bacc
    from concourse.bass_utils import run_bass_kernel_spmd

    nc = bacc.Bacc("TRN2", target_bir_lowering=False, num_devices=1)
    arrays = {}

    def given(name, a):
        a = np.ascontiguousarray(a)
        arrays[f"in_{name}"] = a
        return nc.dram_tensor(f"in_{name}", a.shape, mybir.dt.from_np(a.dtype), kind="ExternalInput").ap()

    ids = np.asarray(inputs["ids"])
    w1 = np.asarray(inputs["W_top1"])
    place = {}
    for a in range(NODES):
        for b in range(a + 1, NODES):
            place[a, b] = D + pair_start(a) + b - a - 1
    pair_rows = [place[min(ORDER[a], ORDER[b]), max(ORDER[a], ORDER[b])]
                 for a in range(NODES) for b in range(a + 1, NODES)]
    w1_order = list(range(D)) + pair_rows + list(range(D + NPAIRS, 2 * D + NPAIRS))
    build(
        nc,
        given("dense_cols", np.asarray(inputs["r_dense_features"]).reshape(TILES, BLOCK, QUAD, D)
              .transpose(3, 0, 2, 1).reshape(D, B)),
        given("ids_rows", ids[:, ONE_HOT].reshape(GROUPS, GROUP, NO).transpose(0, 2, 1)),
        given("ids_cols", ids[:, GATHERED].reshape(TILES, TILE, NG).transpose(1, 0, 2).reshape(TILE, TILES * NG)),
        [given(f"tbl_{f}", inputs[f"tbl_{f}"]) for f in range(TABLES)],
        given("w1", w1[w1_order]),
        given("w2", inputs["W_top2"]),
        given("vectors", np.concatenate([np.asarray(inputs[n]).reshape(-1, P).T
                                         for n in ("b_top1", "b_top2", "W_top3")], axis=1)),
        nc.dram_tensor("out_y", (B, 1), F32, kind="ExternalOutput").ap(),
    )
    return run_bass_kernel_spmd(nc, [arrays], core_ids=[0]).results[0]["out_y"]
```
